# Optimizing a Trainium2 kernel written in Bass

```python
import numpy as np
import jax
import jax.numpy as jnp

def _softmax(x, axis=-1):
    return jax.nn.softmax(x, axis=axis)

def _gelu(x):
    return jax.nn.gelu(x, approximate=True)

def _silu(x):
    return jax.nn.silu(x)

def _sigmoid(x):
    return jax.nn.sigmoid(x)

def _layernorm(x, axis=-1, eps=1e-05):
    m = jnp.mean(x, axis=axis, keepdims=True)
    v = jnp.var(x, axis=axis, keepdims=True)
    return (x - m) / jnp.sqrt(v + eps)

def _scatter_add(tgt, idx, src, axis=0):
    return tgt.at[idx].add(src)

def _segment_sum(src, seg, n):
    return jax.ops.segment_sum(src, seg, n)
kernel_name = 'mk_adj_resnorm_d4_adj_r2_96b937'

def setup_inputs(seed: int=0):
    np.random.seed(seed)
    _w = jnp.asarray

    def _rec_inputs():
        import jax
        import jax.numpy as jnp
        _gk = jax.random.key(seed)
        x = -0.0002928 + 1 * jax.random.normal(jax.random.fold_in(_gk, 1), (128, 64, 256), jnp.float32)
        _a = jax.random.bernoulli(jax.random.fold_in(_gk, 2), 0.0625, (128, 64, 64))
        _a = jnp.logical_or(_a, jnp.eye(64, dtype=bool))
        adj = _a.astype(jnp.int32)
        return (x, adj)
    x, adj = _rec_inputs()

    def _L0_gnn_setup():
        import jax, jax.numpy as jnp
        import numpy as np
        B, N, D = (8, 512, 256)
        NH = 8
        DK = D // NH
        key = jax.random.key(seed)
        ks = jax.random.split(key, 6)
        x = jax.random.normal(ks[0], (B, N, D), dtype=jnp.float32)
        adj = jax.random.randint(ks[1], (B, N, N), 0, 2, dtype=jnp.int32)
        adj = jnp.maximum(adj, jnp.eye(N, dtype=jnp.int32)[None])
        s = 1.0 / np.sqrt(D)
        Wq = jax.random.normal(ks[2], (D, D), dtype=jnp.float32) * s
        Wk = jax.random.normal(ks[3], (D, D), dtype=jnp.float32) * s
        Wv = jax.random.normal(ks[4], (D, D), dtype=jnp.float32) * s
        Wo = jax.random.normal(ks[5], (D, D), dtype=jnp.float32) * s
        return {'x': x, 'adj': adj, 'Wq': Wq, 'Wk': Wk, 'Wv': Wv, 'Wo': Wo}
    _L0_gnn_all = _L0_gnn_setup()
    _L0_gnn_in = {k: v for k, v in _L0_gnn_all.items() if k in ('Wq', 'Wk', 'Wv', 'Wo')}
    del _L0_gnn_all

    def _L1_gnn_setup():
        import jax, jax.numpy as jnp
        import numpy as np
        ALPHA = 0.2

        def _leaky(x):
            return jnp.where(x >= 0, x, ALPHA * x)
        key = jax.random.key(seed)
        k1, k2, k3, k4 = jax.random.split(key, 4)
        B, N, F_in, F_out = (4, 1024, 256, 256)
        h = jax.random.normal(k1, (B, N, F_in), dtype=jnp.float32)
        W = jax.random.normal(k2, (F_in, F_out), dtype=jnp.float32) * 0.05
        a = jax.random.normal(k3, (2 * F_out, 1), dtype=jnp.float32) * 0.05
        adj = jax.random.randint(k4, (B, N, N), 0, 2, dtype=jnp.int32)
        return {'h': h, 'W': W, 'a': a, 'adj': adj}
    _L1_gnn_all = _L1_gnn_setup()
    _L1_gnn_in = {k: v for k, v in _L1_gnn_all.items() if k in ('W', 'a')}
    del _L1_gnn_all

    def _L2_gnn_setup():
        import jax, jax.numpy as jnp
        import numpy as np
        B, N, DIN, DOUT = (8, 1024, 256, 256)
        key = jax.random.key(seed)
        kx, ka, kw, kb, kattn = jax.random.split(key, 5)
        x = jax.random.normal(kx, (B, N, DIN), dtype=jnp.float32)
        adjacency_matrix = jax.random.randint(ka, (B, N, N), 0, 2, dtype=jnp.int32)
        lim_w = float(np.sqrt(1.0 / DIN))
        W = jax.random.uniform(kw, (DOUT, DIN), minval=-lim_w, maxval=lim_w, dtype=jnp.float32)
        b = jax.random.uniform(kb, (DOUT,), minval=-lim_w, maxval=lim_w, dtype=jnp.float32)
        lim_a = float(np.sqrt(6.0 / (DOUT + DOUT)))
        attn = jax.random.uniform(kattn, (DOUT, DOUT), minval=-lim_a, maxval=lim_a, dtype=jnp.float32)
        return {'x': x, 'adjacency_matrix': adjacency_matrix, 'W': W, 'b': b, 'attn': attn}
    _L2_gnn_all = _L2_gnn_setup()
    _L2_gnn_in = {k: v for k, v in _L2_gnn_all.items() if k in ('W', 'b', 'attn')}
    del _L2_gnn_all

    def _L3_gnn_setup():
        import jax, jax.numpy as jnp
        import numpy as np
        L = 3
        D = 256
        B, N = (8, 512)
        EPS = 1e-05

        def layernorm(x, gamma, beta):
            mu = jnp.mean(x, axis=-1, keepdims=True)
            var = jnp.var(x, axis=-1, keepdims=True)
            return (x - mu) * jax.lax.rsqrt(var + EPS) * gamma + beta
        key = jax.random.key(seed)
        ks = jax.random.split(key, 12)
        s = 1.0 / np.sqrt(D)
        node_features = jax.random.normal(ks[0], (B, N, D), dtype=jnp.float32)
        adjacency_matrix = jax.random.randint(ks[1], (B, N, N), 0, 2, dtype=jnp.int32)
        return {'node_features': node_features, 'adjacency_matrix': adjacency_matrix, 'attn_w': jax.random.normal(ks[2], (L, 2 * D), dtype=jnp.float32) * (1.0 / np.sqrt(2 * D)), 'attn_b': jax.random.normal(ks[3], (L,), dtype=jnp.float32) * 0.01, 'W1': jax.random.normal(ks[4], (L, D, 4 * D), dtype=jnp.float32) * s, 'b1': jnp.zeros((L, 4 * D), dtype=jnp.float32), 'W2': jax.random.normal(ks[5], (L, 4 * D, D), dtype=jnp.float32) * (1.0 / np.sqrt(4 * D)), 'b2': jnp.zeros((L, D), dtype=jnp.float32), 'g1': jnp.ones((L, D), dtype=jnp.float32), 'beta1': jnp.zeros((L, D), dtype=jnp.float32), 'g2': jnp.ones((L, D), dtype=jnp.float32), 'beta2': jnp.zeros((L, D), dtype=jnp.float32)}
    _L3_gnn_all = _L3_gnn_setup()
    _L3_gnn_in = {k: v for k, v in _L3_gnn_all.items() if k in ('attn_w', 'attn_b', 'W1', 'b1', 'W2', 'b2', 'g1', 'beta1', 'g2', 'beta2')}
    del _L3_gnn_all
    return {'x': x, 'adj': adj, 'L0_gnn_Wq': _L0_gnn_in['Wq'], 'L0_gnn_Wk': _L0_gnn_in['Wk'], 'L0_gnn_Wv': _L0_gnn_in['Wv'], 'L0_gnn_Wo': _L0_gnn_in['Wo'], 'L1_gnn_W': _L1_gnn_in['W'], 'L1_gnn_a': _L1_gnn_in['a'], 'L2_gnn_W': _L2_gnn_in['W'], 'L2_gnn_b': _L2_gnn_in['b'], 'L2_gnn_attn': _L2_gnn_in['attn'], 'L3_gnn_attn_w': _L3_gnn_in['attn_w'], 'L3_gnn_attn_b': _L3_gnn_in['attn_b'], 'L3_gnn_W1': _L3_gnn_in['W1'], 'L3_gnn_b1': _L3_gnn_in['b1'], 'L3_gnn_W2': _L3_gnn_in['W2'], 'L3_gnn_b2': _L3_gnn_in['b2'], 'L3_gnn_g1': _L3_gnn_in['g1'], 'L3_gnn_beta1': _L3_gnn_in['beta1'], 'L3_gnn_g2': _L3_gnn_in['g2'], 'L3_gnn_beta2': _L3_gnn_in['beta2']}

def reference(x, adj, L0_gnn_Wq, L0_gnn_Wk, L0_gnn_Wv, L0_gnn_Wo, L1_gnn_W, L1_gnn_a, L2_gnn_W, L2_gnn_b, L2_gnn_attn, L3_gnn_attn_w, L3_gnn_attn_b, L3_gnn_W1, L3_gnn_b1, L3_gnn_W2, L3_gnn_b2, L3_gnn_g1, L3_gnn_beta1, L3_gnn_g2, L3_gnn_beta2):
    import jax
    import jax.numpy as jnp

    def _L0_gnn_ref(x, adj, Wq, Wk, Wv, Wo):
        import jax, jax.numpy as jnp
        import numpy as np
        B, N, D = (8, 512, 256)
        NH = 8
        DK = D // NH
        b, n, d = x.shape
        sqrt_dk = jnp.asarray(np.sqrt(DK), dtype=x.dtype)

        def heads(t):
            return t.reshape(b, n, NH, DK).transpose(0, 2, 1, 3)
        q = heads(x @ Wq)
        k = heads(x @ Wk)
        v = heads(x @ Wv)
        scores = jnp.einsum('bhnd,bhmd->bhnm', q, k) / sqrt_dk
        mask = adj.astype(bool)[:, None]
        scores = jnp.where(mask, scores, -jnp.inf)
        attn = jax.nn.softmax(scores, axis=-1)
        out = jnp.einsum('bhnm,bhmd->bhnd', attn, v)
        out = out.transpose(0, 2, 1, 3).reshape(b, n, d)
        return jax.nn.relu(out) @ Wo

    def _L1_gnn_ref(h, W, a, adj):
        import jax, jax.numpy as jnp
        import numpy as np
        ALPHA = 0.2

        def _leaky(x):
            return jnp.where(x >= 0, x, ALPHA * x)
        F_out = W.shape[1]
        Wh = jnp.matmul(h, W)
        Wh_sg = jax.lax.stop_gradient(Wh)
        a1 = a[:F_out, 0]
        a2 = a[F_out:, 0]
        s_i = Wh_sg @ a1
        s_j = Wh_sg @ a2
        e = _leaky(s_i[:, :, None] + s_j[:, None, :])
        e = jnp.where(adj > 0, e, jnp.float32(-9000000000000000.0))
        attention = jax.nn.softmax(e, axis=1)
        h_prime = jnp.einsum('bij,bjf->bif', attention, Wh)
        return _leaky(h_prime)

    def _L2_gnn_ref(x, adjacency_matrix, W, b, attn):
        import jax, jax.numpy as jnp
        import numpy as np
        B, N, DIN, DOUT = (8, 1024, 256, 256)
        h = jnp.einsum('bni,oi->bno', x, W) + b
        ha = jnp.einsum('bmi,ij->bmj', h, attn)
        scores = jnp.einsum('bmj,bnj->bmn', ha, h)
        scores = jnp.where(adjacency_matrix == 0, -jnp.inf, scores)
        attn_weights = jax.nn.softmax(scores, axis=-1)
        x_out = jnp.einsum('bmn,bnd->bmd', attn_weights, h)
        return jax.nn.elu(x_out)

    def _L3_gnn_ref(node_features, adjacency_matrix, attn_w, attn_b, W1, b1, W2, b2, g1, beta1, g2, beta2):
        import jax, jax.numpy as jnp
        import numpy as np
        L = 3
        D = 256
        B, N = (8, 512)
        EPS = 1e-05

        def layernorm(x, gamma, beta):
            mu = jnp.mean(x, axis=-1, keepdims=True)
            var = jnp.var(x, axis=-1, keepdims=True)
            return (x - mu) * jax.lax.rsqrt(var + EPS) * gamma + beta
        n = adjacency_matrix.shape[-1]
        mask = adjacency_matrix.astype(jnp.float32) + jnp.eye(n, dtype=jnp.float32) > 0
        x = node_features
        d = x.shape[-1]
        for l in range(attn_w.shape[0]):
            si = x @ attn_w[l, :d]
            sj = x @ attn_w[l, d:]
            scores = si[:, :, None] + sj[:, None, :] + attn_b[l]
            scores = jnp.where(scores >= 0, scores, 0.2 * scores)
            scores = jnp.where(mask, scores, -jnp.inf)
            attn = jax.nn.softmax(scores, axis=-1)
            agg = jnp.einsum('bij,bjd->bid', attn, x)
            h = layernorm(x + agg, g1[l], beta1[l])
            ff = jax.nn.gelu(h @ W1[l] + b1[l], approximate=False) @ W2[l] + b2[l]
            x = layernorm(h + ff, g2[l], beta2[l])
        return x
    x = _layernorm(x + _L0_gnn_ref(x, adj, L0_gnn_Wq, L0_gnn_Wk, L0_gnn_Wv, L0_gnn_Wo), axis=-1)
    x = _layernorm(x + _L1_gnn_ref(x, L1_gnn_W, L1_gnn_a, adj), axis=-1)
    x = _layernorm(x + _L2_gnn_ref(x, adj, L2_gnn_W, L2_gnn_b, L2_gnn_attn), axis=-1)
    x = _layernorm(x + _L3_gnn_ref(x, adj, L3_gnn_attn_w, L3_gnn_attn_b, L3_gnn_W1, L3_gnn_b1, L3_gnn_W2, L3_gnn_b2, L3_gnn_g1, L3_gnn_beta1, L3_gnn_g2, L3_gnn_beta2), axis=-1)
    return x

_drawn_inputs = setup_inputs


def setup_inputs(seed=0):
    import zlib

    import numpy as np

    out = dict(_drawn_inputs(seed))
    spreads = {'L3_gnn_b1': (0.0, 0.1),
     'L3_gnn_b2': (0.0, 0.1),
     'L3_gnn_g1': (1.0, 0.2),
     'L3_gnn_beta1': (0.0, 0.1),
     'L3_gnn_g2': (1.0, 0.2),
     'L3_gnn_beta2': (0.0, 0.1)}
    factors = {'L3_gnn_attn_b': 64.0}
    for name, (base, spread) in spreads.items():
        noise = np.random.default_rng([zlib.crc32(name.encode()), seed]).standard_normal(out[name].shape)
        drawn = base * np.exp(spread * noise) if base else spread * noise
        out[name] = jnp.asarray(drawn.astype(out[name].dtype))
    for name, factor in factors.items():
        out[name] = (out[name] * factor).astype(out[name].dtype)
    return out
```

```python
from contextlib import ExitStack

import concourse.bass as bass
from concourse import mybir

F32 = mybir.dt.float32
F32R = mybir.dt.float32r
I32 = mybir.dt.int32
ALU = mybir.AluOpType
ACT = mybir.ActivationFunctionType
AX_X = mybir.AxisListType.X

P = 128
D = 256
KC = D // P
N = 64
TILES = 2
R = TILES * P
NH = 8
DK = D // NH
RG = 4
HC = NH // RG
L = 3
FF = 4 * D
FC = FF // P
EPS = 1e-5
MASKED = -1e30
OTHER = -3e38
MASKED_L1 = -9e15
WQ, WK, WV, WO, W1H, W2T, W2M = range(7)
R_WI, R_G1, R_B1, R_G2, R_B2, R_A2, R_LB = 0, L, 2 * L, 3 * L, 4 * L, 5 * L, 5 * L + 1
ROWS = 5 * L + 2
PHASES = 9


class Stream:
    pass


class Signal:

    def __init__(self, sem, per):
        self.sem, self.per = sem, per

    def at(self, g, k):
        return self.sem, g * self.per + k


def merged(a, b):
    pa, pb = next(a, None), next(b, None)
    while pa is not None or pb is not None:
        if pb is None or (pa is not None and pa <= pb):
            pa = next(a, None)
        else:
            pb = next(b, None)


def gnn_kernel(nc, x, adj, w_small, w1, w2, cols, rows, prep_rows, out):
    groups = x.shape[0] // (2 * R)
    x_v = x.rearrange("(n t p) d -> n p t d", t=TILES, p=P)
    out_v = out.rearrange("(n t p) d -> n p t d", t=TILES, p=P)
    adj_v = adj.rearrange("(n t p) j -> n p t j", t=TILES, p=P)
    C_FB, C_BETA1, C_G1, C_WJ, C_LB, C_AB = 0, L * FC, L * FC + L * KC, L * FC + 2 * L * KC, L * FC + 3 * L * KC, L * FC + 3 * L * KC + KC
    NCOLS = C_AB + L

    with ExitStack() as ctx:
        def sb(name, shape, dt=F32):
            return ctx.enter_context(nc.sbuf_tensor(name, shape, dt))

        def sem(name):
            return ctx.enter_context(nc.semaphore(name))

        ws_h = sb("ws_h", [P, 7, KC, D], F32R)
        ws_l = sb("ws_l", [P, 7, KC, D], F32R)
        w1_h = sb("w1_h", [P, L, KC, FF], F32R)
        w1_l = sb("w1_l", [P, L, KC, FF], F32R)
        w2_h = sb("w2_h", [P, L, FC, D], F32R)
        w2_l = sb("w2_l", [P, L, FC, D], F32R)
        rep_h = sb("rep_h", [P, 1 + L, KC, P], F32R)
        rep_l = sb("rep_l", [P, 1 + L, KC, P], F32R)
        col = sb("col", [P, NCOLS])
        row = sb("row", [P, ROWS, D])
        ident = sb("ident", [P, P])
        eye = sb("eye", [P, N])
        ffb = sb("ffb", [P, L * FC])
        mcol = sb("mcol", [P, KC])
        wa1 = sb("wa1", [P, KC])
        other = sb("other", [P, 2])
        epst = sb("epst", [P, TILES])
        mhalf = sb("mhalf", [P, TILES])
        g_hi = sb("g_hi", [P, 2, R], F32R)
        g_lo = sb("g_lo", [P, 2, R], F32R)

        w_in = [sem(f"w_in{i}") for i in range(2)]
        c_in = sem("c_in")
        ones_ready = sem("ones_ready")
        ident_ready = sem("ident_ready")
        w_hi = sem("w_hi")
        w_lo = sem("w_lo")
        w_used = sem("w_used")
        prep_dve = sem("prep_dve")
        prep_act = sem("prep_act")
        prep_pe = sem("prep_pe")
        consts = sem("consts")
        gate = {name: sem(f"gate_{name}") for name in ("pe", "dve", "pool", "sp")}
        ff_act = Signal(sem("ff_gelu"), FC)
        ff_hi = Signal(sem("ff_hi"), FC)
        ff_lo = Signal(sem("ff_lo"), FC)
        ff_used = Signal(sem("ff_used"), FC)

        streams = []
        for s in range(2):
            q = Stream()
            q.sig = {name: Signal(sem(f"{name}_{s}"), per) for name, per in dict(
                load=32, out=16, adjf=1, mask=11,
                xt_ps=9, xt_hi=9, xt_lo=9,
                q_ps=1, k_ps=1, v_ps=1, q_sb=1, k_sb=1, v_sb=1, vsw_sb=2,
                s_ps=1, p_add=2, p_max=2, p_sub=2, p_exp=2, p_sum=2, p_inv=2, p_norm=2,
                pt0_ps=2, pt0_sb=2, pv0_ps=2, o_hi=1, o_lo=1, y_ps=1,
                negt_ps=1, lin_ps=4, wh_ps=1, wh_sb=1, sc_dot=8, sc_ready=3, lin=8,
                h_ps=3, h_sb=2, ha_sb=2, hrow_sb=1, sc_ps=1,
                e_add=5, e_max=5, e_exp=10, e_inv=5, e_norm=2,
                pt_ps=4, pt_sb=4, agg_ps=5, leaky=1, h1_sb=1, leak=4, elu_y=2, elu_m=1, elu_e=1, elu_s=1,
                u=10, st=20, mv=20, ve=10, rstd=10, z=20,
                hb1=3, hb=3, f_ps=24, u_b=3, aff1=3, aff=3,
            ).items()}
            q.s = s
            q.xin = sb(f"xin{s}", [P, TILES, D])
            q.xrow = sb(f"xrow{s}", [P, TILES, D])
            q.u_sb = sb(f"u{s}", [P, TILES, D])
            q.xkeep = sb(f"xkeep{s}", [P, TILES, D])
            q.xt_h = sb(f"xt_h{s}", [P, KC, R], F32R)
            q.xt_l = sb(f"xt_l{s}", [P, KC, R], F32R)
            q.val = sb(f"val{s}", [P, TILES, D])
            q.val_sw = sb(f"val_sw{s}", [P, TILES, D])
            q.work = sb(f"work{s}", [P, 4, R])
            q.pt = sb(f"pt{s}", [P, 4 * P])
            q.adji = sb(f"adji{s}", [P, TILES, N], I32)
            q.adjf_sb = sb(f"adjf{s}", [P, TILES, N])
            q.negc = sb(f"negc{s}", [P, TILES, N])
            q.neg1 = sb(f"neg1{s}", [P, TILES, P])
            q.negm = sb(f"negm{s}", [P, TILES, P])
            q.mx = sb(f"mx{s}", [P, NH * TILES])
            q.sm = sb(f"sm{s}", [P, NH * TILES])
            q.stat = sb(f"stat{s}", [P, TILES, 6])
            q.mv_sb = sb(f"mv{s}", [P, TILES, 2])
            q.ve_sb = sb(f"ve{s}", [P, TILES])
            q.rstd_sb = sb(f"rstd{s}", [P, TILES])
            q.sc = sb(f"sc{s}", [P, TILES])
            q.bank = ctx.enter_context(nc.psum_tensor(f"bank{s}", [P, 4, 512], F32))
            q.scores = q.pt[:, 2 * P:].rearrange("p (t j) -> p t j", t=TILES)
            streams.append(q)

        def f32(ap):
            return ap.bitcast(F32)

        def split3(pe, out_ap, lh, ll, rh, rl, first, last, start=True):
            pe.matmul(out_ap, lh, rh, start=first and start, stop=False, skip_group_check=True)
            pe.matmul(out_ap, lh, rl, start=False, stop=False, skip_group_check=True)
            return pe.matmul(out_ap, ll, rh, start=False, stop=last, skip_group_check=True)

        stage = [streams[u].work[:].rearrange("p a b -> p (a b)") for u in range(2)]
        units = [("small", i) for i in range(3)] + [("mix", 0)] + [("w1", l, k) for l in range(L) for k in range(KC)] \
            + [("w2", l, h) for l in range(L) for h in range(2)]

        block = ctx.enter_context(nc.Block())

        def unit_src(u):
            if u[0] in ("small", "mix"):
                i = u[1] if u[0] == "small" else 3
                return w_small[i].rearrange("(m k p) n -> p m k n", m=2, p=P), "p (m k n) -> p m k n", dict(m=2, k=KC)
            if u[0] == "w1":
                return w1[u[1], u[2] * P:(u[2] + 1) * P, :], None, None
            return w2[u[1], u[2] * 512:(u[2] + 1) * 512, :].rearrange("(f p) d -> p f d", p=P), "p (f d) -> p f d", dict(f=4)

        def unit_dst(u, part):
            ws, wa, wb = (ws_h, w1_h, w2_h) if part == "hi" else (ws_l, w1_l, w2_l)
            if u[0] == "small":
                return ws[:, 2 * u[1]:2 * u[1] + 2, :, :].rearrange("p m k n -> p (m k n)")
            if u[0] == "w1":
                return wa[:, u[1], u[2], :]
            return wb[:, u[1], 4 * u[2]:4 * u[2] + 4, :].rearrange("p f d -> p (f d)")

        def prep_sync(sp):
            sp.dma_start(col[:, :], cols).then_inc(c_in, 16)
            sp.dma_start(row[:, :, :], rows.partition_broadcast(P)).then_inc(c_in, 16)
            sp.dma_start(streams[0].xrow[:, 0, :], prep_rows[0].partition_broadcast(P)).then_inc(c_in, 16)
            sp.dma_start(streams[0].val[:, :, :], prep_rows[1:3].partition_broadcast(P)).then_inc(c_in, 16)
            sp.dma_start(streams[0].val_sw[:, 0, :], prep_rows[3].partition_broadcast(P)).then_inc(c_in, 16)
            for i, u in enumerate(units):
                src, pat, kw = unit_src(u)
                if i >= 2:
                    sp.wait_ge(w_lo, i - 1)
                    if 3 <= i - 2 < 4 + L * KC:
                        sp.wait_ge(w_used, i - 4)
                dst = stage[i % 2] if pat is None else stage[i % 2].rearrange(pat, **kw)
                sp.dma_start(dst, src).then_inc(w_in[i % 2], 16)

        def prep_scalar(act):
            act.wait_ge(c_in, 80)
            for i, u in enumerate(units):
                act.wait_ge(w_in[i % 2], 16 * (i // 2 + 1))
                if u[0] == "mix":
                    act.wait_ge(prep_pe, 1)
                    act.activation(ws_h[:, W2M, :, :].rearrange("p k n -> p (k n)"), streams[0].bank[:, 0, :], ACT.Copy).then_inc(w_hi, 1)
                elif u[0] == "w1":
                    c = C_G1 + u[1] * KC + u[2]
                    act.activation(unit_dst(u, "hi"), stage[i % 2], ACT.Copy, scale=col[:, c:c + 1]).then_inc(w_hi, 1)
                else:
                    act.activation(unit_dst(u, "hi"), stage[i % 2], ACT.Copy).then_inc(w_hi, 1)

        def prep_vector(dve):
            dve.wait_ge(c_in, 80)
            n = 0
            for b in range(2):
                dve.memset(other[b * N:(b + 1) * N, b:b + 1], 0.0).then_inc(prep_dve, 1)
                dve.memset(other[b * N:(b + 1) * N, 1 - b:2 - b], OTHER).then_inc(prep_dve, 1)
                n += 2
            dve.memset(epst[:, :], EPS).then_inc(prep_dve, 1)
            dve.memset(mhalf[:, :], -0.5).then_inc(prep_dve, 1)
            ones = streams[0].pt[:, 0:P]
            dve.memset(ones, 1.0).then_inc(prep_dve, 1)
            n += 3
            dve.tensor_tensor(row[:, R_B1:R_B1 + 2, :], row[:, R_B1:R_B1 + 2, :], streams[0].val[:, :, :], ALU.add).then_inc(prep_dve, 1)
            dve.tensor_tensor(row[:, R_B1 + 2, :], row[:, R_B1 + 2, :], streams[0].val_sw[:, 0, :], ALU.add).then_inc(prep_dve, 1)
            n += 2
            for i, u in enumerate(units):
                raw = stage[i % 2]
                dve.wait_ge(w_in[i % 2], 16 * (i // 2 + 1))
                dve.wait_ge(w_hi, i + 1)
                if u == ("small", 2):
                    for k in range(KC):
                        dve.wait_ge(prep_dve, n)
                        dve.tensor_tensor_reduce(out=streams[0].u_sb[:, 0, :], in0=raw[:, k * D:(k + 1) * D], in1=streams[0].xrow[:, 0, :],
                                                 scale=1.0, scalar=0.0, op0=ALU.mult, op1=ALU.add,
                                                 accum_out=wa1[:, k:k + 1]).then_inc(prep_dve, 1)
                        n += 1
                if u[0] == "mix":
                    dve.tensor_tensor(ws_l[:, W2M, :, :].rearrange("p k n -> p (k n)"), streams[0].bank[:, 0, :],
                                      f32(ws_h[:, W2M, :, :]).rearrange("p k n -> p (k n)"), ALU.subtract).then_inc(w_lo, 1)
                elif u[0] == "w1":
                    c = C_G1 + u[1] * KC + u[2]
                    dve.scalar_tensor_tensor(out=unit_dst(u, "lo"), in0=raw, scalar=col[:, c:c + 1], in1=f32(unit_dst(u, "hi")),
                                             op0=ALU.mult, op1=ALU.subtract).then_inc(w_lo, 1)
                else:
                    dve.tensor_tensor(unit_dst(u, "lo"), raw, f32(unit_dst(u, "hi")), ALU.subtract).then_inc(w_lo, 1)
            dve.wait_ge(prep_dve, n)
            for m in range(1 + L):
                for k in range(KC):
                    c = wa1[:, k:k + 1] if m == 0 else col[:, C_WJ + (m - 1) * KC + k:C_WJ + (m - 1) * KC + k + 1]
                    dve.tensor_scalar(rep_h[:, m, k, :], ones, c, None, ALU.mult).then_inc(prep_dve, 1)
                    n += 1
                    dve.wait_ge(prep_dve, n)
                    dve.scalar_tensor_tensor(out=rep_l[:, m, k, :], in0=ones, scalar=c, in1=f32(rep_h[:, m, k, :]),
                                             op0=ALU.mult, op1=ALU.subtract).then_inc(prep_dve, 1)
                    n += 1
            dve.wait_ge(w_used, 1)
            dve.tensor_copy(mcol[:, :], streams[0].bank[:, 1, 0:KC]).then_inc(prep_dve, 1)
            dve.wait_ge(w_used, 1 + L * KC)
            dve.tensor_tensor(ffb[:, :], streams[1].bank[:, 0, 0:L * FC], col[:, C_FB:C_FB + L * FC], ALU.add).then_inc(prep_dve, 1)
            n += 2
            dve.wait_ge(prep_dve, n)
            dve.engine_nop().then_inc(consts, 1)

        def prep_tensor(pe):
            pe.wait_ge(c_in, 80)
            for i, u in enumerate(units):
                raw = stage[i % 2]
                pe.wait_ge(w_in[i % 2], 16 * (i // 2 + 1))
                if u[0] == "mix":
                    m = raw.rearrange("p (m k n) -> p m k n", m=2, k=KC)
                    for i2 in range(KC):
                        for o in range(KC):
                            ins = pe.matmul(streams[0].bank[:, 0, i2 * D:(i2 + 1) * D], m[:, 0, o, i2 * P:(i2 + 1) * P], m[:, 1, o, :],
                                            start=(o == 0), stop=(o == KC - 1))
                    ins.then_inc(prep_pe, 1)
                    for j in range(KC):
                        for o in range(KC):
                            ins = pe.matmul(streams[0].bank[:, 1, j:j + 1], m[:, 1, o, j * P:(j + 1) * P], col[:, C_LB + o:C_LB + o + 1],
                                            start=(o == 0), stop=(o == KC - 1))
                    ins.then_inc(w_used, 1)
                elif u[0] == "w1":
                    _, l, k = u
                    for f in range(FC):
                        ins = pe.matmul(streams[1].bank[:, 0, l * FC + f:l * FC + f + 1], raw[:, f * P:(f + 1) * P],
                                        col[:, C_BETA1 + l * KC + k:C_BETA1 + l * KC + k + 1],
                                        start=(l == 0 and k == 0 and f == 0), stop=(k == KC - 1), skip_group_check=True)
                    ins.then_inc(w_used, 1)

        def prep_gpsimd(pool):
            pool.memset(ident[:, :], 0.0).then_inc(ones_ready, 1)
            pool.memset(eye[:, :], 0.0).then_inc(ones_ready, 1)
            pool.wait_ge(ones_ready, 2)
            pool.affine_select(out=ident[:, :], in_=ident[:, :], compare_op=ALU.not_equal, fill=1.0, base=0,
                               pattern=[[-1, P]], channel_multiplier=1).then_inc(ident_ready, 1)
            pool.affine_select(out=eye[:, :], in_=eye[:, :], compare_op=ALU.not_equal, fill=1.0, base=0,
                               pattern=[[-1, N]], channel_multiplier=1).then_inc(ident_ready, 1)
            pool.wait_ge(ident_ready, 2)
            pool.affine_select(out=eye[:, :], in_=eye[:, :], compare_op=ALU.not_equal, fill=1.0, base=-N,
                               pattern=[[-1, N]], channel_multiplier=1).then_inc(ident_ready, 1)
            pool.wait_ge(ident_ready, 3)

        def pe_xt(pe, q, g, n, src):
            for k in range(KC):
                for t in range(TILES):
                    ins = pe.transpose(q.bank[:, 0, k * R + t * P:k * R + (t + 1) * P], src[:, t, k * P:(k + 1) * P], ident[:, :])
            ins.then_inc(q.sig["xt_ps"].sem, 1)

        def act_xt(act, q, g, n):
            act.wait_ge(*q.sig["xt_ps"].at(g, n + 1))
            act.activation(q.xt_h[:, :, :].rearrange("p k r -> p (k r)"), q.bank[:, 0, :], ACT.Copy).then_inc(q.sig["xt_hi"].sem, 1)

        def dve_xt(dve, q, g, n):
            dve.wait_ge(*q.sig["xt_hi"].at(g, n + 1))
            dve.tensor_tensor(q.xt_l[:, :, :].rearrange("p k r -> p (k r)"), q.bank[:, 0, :],
                              f32(q.xt_h[:, :, :]).rearrange("p k r -> p (k r)"), ALU.subtract).then_inc(q.sig["xt_lo"].sem, 1)

        def pe_rows(pe, q, bank, w, lh=None):
            for t in range(TILES):
                for k in range(KC):
                    ins = split3(pe, q.bank[:, bank, t * D:(t + 1) * D], q.xt_h[:, k, t * P:(t + 1) * P], q.xt_l[:, k, t * P:(t + 1) * P],
                                 ws_h[:, w, k, :], ws_l[:, w, k, :], k == 0, k == KC - 1)
            return ins

        def pe_cols(pe, q, bank, w):
            for o in range(KC):
                for k in range(KC):
                    ins = split3(pe, q.bank[:, bank, o * R:(o + 1) * R], ws_h[:, w, k, o * P:(o + 1) * P], ws_l[:, w, k, o * P:(o + 1) * P],
                                 q.xt_h[:, k, :], q.xt_l[:, k, :], k == 0, k == KC - 1)
            return ins

        def pe_rep(pe, q, m):
            for k in range(KC):
                ins = split3(pe, q.bank[:, 1, 0:R], rep_h[:, m, k, :], rep_l[:, m, k, :], q.xt_h[:, k, :], q.xt_l[:, k, :], k == 0, k == KC - 1)
            ins.then_inc(q.sig["lin_ps"].sem, 1)

        def dve_norm(dve, q, g, n, dst):
            dve.wait_ge(*q.sig["u"].at(g, n + 1))
            for t in range(TILES):
                dve.bn_stats(q.stat[:, t, :], q.u_sb[:, t, :]).then_inc(q.sig["st"].sem, 1)
            for t in range(TILES):
                dve.wait_ge(*q.sig["st"].at(g, TILES * n + t + 1))
                dve.sem_inc(gate["dve"], 1)
                dve.bn_aggr(q.mv_sb[:, t, :], q.stat[:, t, :]).then_inc(q.sig["mv"].sem, 1)
            dve.wait_ge(*q.sig["rstd"].at(g, n + 1))
            for t in range(TILES):
                dve.tensor_scalar(dst[:, t, :], q.u_sb[:, t, :], q.mv_sb[:, t, 0:1], q.rstd_sb[:, t:t + 1],
                                  ALU.subtract, ALU.mult).then_inc(q.sig["z"].sem, 1)

        def pool_norm(pool, q, g, n):
            pool.wait_ge(*q.sig["mv"].at(g, TILES * (n + 1)))
            pool.tensor_tensor(q.ve_sb[:, :], q.mv_sb[:, :, 1], epst[:, :], ALU.add).then_inc(q.sig["ve"].sem, 1)
            pool.wait_ge(*q.sig["ve"].at(g, n + 1))
            pool.tensor_tensor(q.rstd_sb[:, :], q.ve_sb[:, :], mhalf[:, :], ALU.pow).then_inc(q.sig["rstd"].sem, 1)

        def dve_leaky(dve, q, g, n):
            dve.wait_ge(*q.sig["lin"].at(g, TILES * (n + 1)))
            dve.scalar_tensor_tensor(out=q.scores[:, :, :], in0=q.scores[:, :, :], scalar=0.2, in1=q.scores[:, :, :],
                                     op0=ALU.mult, op1=ALU.max).then_inc(q.sig["leak"].sem, 1)
            dve.wait_ge(*q.sig["leak"].at(g, n + 1))

        def dve_mask_max(dve, q, g, n, scores, neg):
            dve.tensor_tensor(q.scores[:, :, :], scores, neg, ALU.add).then_inc(q.sig["e_add"].sem, 1)
            dve.wait_ge(*q.sig["e_add"].at(g, n + 1))
            dve.tensor_reduce(q.mx[:, 0:TILES], q.scores[:, :, :], AX_X, ALU.max, negate=True).then_inc(q.sig["e_max"].sem, 1)

        def act_exp(act, q, g, n):
            act.wait_ge(*q.sig["e_max"].at(g, n + 1))
            for t in range(TILES):
                act.activation(q.scores[:, t, :], q.scores[:, t, :], ACT.Exp, bias=q.mx[:, t:t + 1],
                               accum_out=q.sm[:, t:t + 1]).then_inc(q.sig["e_exp"].sem, 1)

        def dve_inv(dve, q, g, n):
            dve.wait_ge(*q.sig["e_exp"].at(g, TILES * (n + 1)))
            dve.reciprocal(q.sm[:, 0:TILES], q.sm[:, 0:TILES]).then_inc(q.sig["e_inv"].sem, 1)

        def pe_pt(pe, q, g, n, bank):
            pe.wait_ge(*q.sig["e_exp"].at(g, TILES * (n + 1)))
            for t in range(TILES):
                ins = pe.transpose(q.bank[:, bank, t * P:(t + 1) * P], q.scores[:, t, :], ident[:, :])
            ins.then_inc(q.sig["pt_ps"].sem, 1)

        def act_pt(act, q, g, n, bank):
            act.wait_ge(*q.sig["pt_ps"].at(g, n))
            act.activation(q.pt[:, 0:TILES * P], q.bank[:, bank, 0:TILES * P], ACT.Copy).then_inc(q.sig["pt_sb"].sem, 1)

        def pe_agg(pe, q, bank, lhs, rhs):
            for t in range(TILES):
                ins = pe.matmul(q.bank[:, bank, t * D:(t + 1) * D], lhs[:, t * P:(t + 1) * P], rhs[:, t, :], start=True, stop=True)
            ins.then_inc(q.sig["agg_ps"].sem, 1)

        def l0_tensor(pe, q, g):
            yield 0.0
            pe.wait_ge(*q.sig["load"].at(g, 32))
            pe_xt(pe, q, g, 0, q.xin)
            yield 0.1
            pe.wait_ge(*q.sig["xt_lo"].at(g, 1))
            pe_cols(pe, q, 1, WQ).then_inc(q.sig["q_ps"].sem, 1)
            yield 0.2
            pe_cols(pe, q, 2, WK).then_inc(q.sig["k_ps"].sem, 1)
            pe_rows(pe, q, 3, WV).then_inc(q.sig["v_ps"].sem, 1)
            yield 0.3
            pe.wait_ge(*q.sig["q_sb"].at(g, 1))
            pe.wait_ge(*q.sig["k_sb"].at(g, 1))
            pe.wait_ge(*q.sig["v_sb"].at(g, 1))
            pe.wait_ge(*q.sig["vsw_sb"].at(g, 2))
            for hc in range(HC):
                for t in range(TILES):
                    for b in range(2):
                        for r in range(RG):
                            c = (t * HC + hc) * N
                            rows_ = slice(t * P + b * N, t * P + (b + 1) * N)
                            ins = pe.matmul(q.bank[b * N:(b + 1) * N, r, c:c + N], q.work[r * DK:(r + 1) * DK, hc, rows_],
                                            q.work[r * DK:(r + 1) * DK, HC + hc, rows_], start=True, stop=True)
            ins.then_inc(q.sig["s_ps"].sem, 1)
            for t in range(TILES):
                yield 0.5 + 0.2 * t
                pe.wait_ge(*q.sig["p_norm"].at(g, t + 1))
                pe.wait_ge(*q.sig["p_add"].at(g, 2))
                for r in range(RG):
                    ins = pe.transpose(q.bank[:, t, r * P:(r + 1) * P], q.work[:, 2 * t + r // 2, (r % 2) * P:(r % 2 + 1) * P], ident[:, :])
                ins.then_inc(q.sig["pt0_ps"].sem, 1)
                yield 0.6 + 0.2 * t
                pe.wait_ge(*q.sig["pt0_sb"].at(g, t + 1))
                pe.sem_inc(gate["pe"], 1)
                for r in range(RG):
                    for b in range(2):
                        for hc in range(HC):
                            v = q.val if b == hc else q.val_sw
                            h = hc * RG + r
                            ins = pe.matmul(q.bank[r * DK:(r + 1) * DK, 2 + hc, t * P + b * N:t * P + (b + 1) * N],
                                            v[hc * N:(hc + 1) * N, t, h * DK:(h + 1) * DK],
                                            q.pt[hc * N:(hc + 1) * N, r * P + b * N:r * P + (b + 1) * N], start=True, stop=True)
                ins.then_inc(q.sig["pv0_ps"].sem, 1)
            yield 0.9
            pe.wait_ge(*q.sig["o_lo"].at(g, 1))
            pe_rows(pe, q, 0, WO).then_inc(q.sig["y_ps"].sem, 1)

        def l0_scalar(act, q, g):
            yield 0.0
            act_xt(act, q, g, 0)
            yield 0.1
            act.wait_ge(*q.sig["q_ps"].at(g, 1))
            act.activation(q.work[:, 0:HC, :].rearrange("p c r -> p (c r)"), q.bank[:, 1, :], ACT.Copy, scale=DK ** -0.5).then_inc(q.sig["q_sb"].sem, 1)
            yield 0.2
            act.wait_ge(*q.sig["v_ps"].at(g, 1))
            act.activation(q.val[:, :, :].rearrange("p t d -> p (t d)"), q.bank[:, 3, :], ACT.Copy).then_inc(q.sig["v_sb"].sem, 1)
            for t in range(TILES):
                yield 0.4 + 0.2 * t
                act.wait_ge(*q.sig["p_sub"].at(g, t + 1))
                p = q.work[:, 2 * t:2 * t + 2, :].rearrange("p c r -> p (c r)")
                act.activation(p, p, ACT.Exp).then_inc(q.sig["p_exp"].sem, 1)
                yield 0.5 + 0.2 * t
                act.wait_ge(*q.sig["pt0_ps"].at(g, t + 1))
                if t:
                    act.wait_ge(*q.sig["pv0_ps"].at(g, t))
                act.activation(q.pt[:, :], q.bank[:, t, :], ACT.Copy).then_inc(q.sig["pt0_sb"].sem, 1)
            yield 0.8
            act.wait_ge(*q.sig["pv0_ps"].at(g, 2))
            act.activation(q.xt_h[:, :, :], q.bank[:, 2:4, 0:R], ACT.Relu).then_inc(q.sig["o_hi"].sem, 1)

        def l0_vector(dve, q, g):
            yield 0.0
            dve_xt(dve, q, g, 0)
            yield 0.2
            dve.wait_ge(*q.sig["k_ps"].at(g, 1))
            dve.tensor_copy(q.work[:, HC:2 * HC, :].rearrange("p c r -> p (c r)"), q.bank[:, 2, :]).then_inc(q.sig["k_sb"].sem, 1)
            dve.wait_ge(*q.sig["v_ps"].at(g, 1))
            dve.wait_ge(*q.sig["v_sb"].at(g, 1))
            for b in range(2):
                dve.tensor_copy(q.val_sw[(1 - b) * N:(2 - b) * N, :, :].rearrange("p t d -> p (t d)"), q.bank[b * N:(b + 1) * N, 3, :]).then_inc(q.sig["vsw_sb"].sem, 1)
            for t in range(TILES):
                yield 0.3 + 0.2 * t
                dve.wait_ge(*q.sig["s_ps"].at(g, 1))
                if t == 0:
                    dve.wait_ge(*q.sig["mask"].at(g, 1))
                p4 = q.work[:, 2 * t:2 * t + 2, :].rearrange("p c (r h j) -> p (c r) h j", r=2, h=HC)
                p = q.work[:, 2 * t:2 * t + 2, :].rearrange("p c (h j) -> p (c h) j", j=N)
                dve.tensor_tensor(p4, q.bank[:, :, t * HC * N:(t + 1) * HC * N].rearrange("p r (h j) -> p r h j", h=HC),
                                  q.negc[:, t:t + 1, :].unsqueeze(1).to_broadcast([P, RG, HC, N]), ALU.add).then_inc(q.sig["p_add"].sem, 1)
                dve.wait_ge(*q.sig["p_add"].at(g, t + 1))
                m = q.mx[:, t * NH:(t + 1) * NH]
                sm = q.sm[:, t * NH:(t + 1) * NH]
                dve.tensor_reduce(m, p, AX_X, ALU.max).then_inc(q.sig["p_max"].sem, 1)
                dve.wait_ge(*q.sig["p_max"].at(g, t + 1))
                dve.tensor_tensor(p, p, m.unsqueeze(2).to_broadcast([P, NH, N]), ALU.subtract).then_inc(q.sig["p_sub"].sem, 1)
                yield 0.4 + 0.2 * t
                dve.wait_ge(*q.sig["p_exp"].at(g, t + 1))
                dve.tensor_reduce(sm, p, AX_X, ALU.add).then_inc(q.sig["p_sum"].sem, 1)
                dve.wait_ge(*q.sig["p_sum"].at(g, t + 1))
                dve.reciprocal(sm, sm).then_inc(q.sig["p_inv"].sem, 1)
                dve.wait_ge(*q.sig["p_inv"].at(g, t + 1))
                dve.tensor_tensor(p, p, sm.unsqueeze(2).to_broadcast([P, NH, N]), ALU.mult).then_inc(q.sig["p_norm"].sem, 1)
            yield 0.8
            dve.wait_ge(*q.sig["o_hi"].at(g, 1))
            dve.scalar_tensor_tensor(out=q.xt_l[:, :, :], in0=q.bank[:, 2:4, 0:R], scalar=0.0, in1=f32(q.xt_h[:, :, :]),
                                     op0=ALU.max, op1=ALU.subtract).then_inc(q.sig["o_lo"].sem, 1)
            yield 0.9
            dve.wait_ge(*q.sig["y_ps"].at(g, 1))
            dve.tensor_tensor(q.u_sb[:, :, :], q.xin[:, :, :], q.bank[:, 0, :].rearrange("p (t d) -> p t d", t=TILES), ALU.add).then_inc(q.sig["u"].sem, 1)
            dve.wait_ge(q.sig["out"].sem, 16 * g + 1)
            dve_norm(dve, q, g, 0, q.xrow)

        def pool_spread(pool, q, neg):
            for b in (1, 0):
                pool.tensor_scalar(neg[:, :, b * N:(b + 1) * N], neg[:, :, 0:N], other[:, b:b + 1], None, ALU.add).then_inc(q.sig["mask"].sem, 1)

        def l0_gpsimd(pool, q, g):
            yield 0.0
            pool.wait_ge(*q.sig["load"].at(g, 32))
            pool.sem_inc(gate["pool"], 1)
            pool.tensor_copy(q.adjf_sb[:, :, :], q.adji[:, :, :]).then_inc(q.sig["adjf"].sem, 1)
            pool.wait_ge(*q.sig["adjf"].at(g, 1))
            pool.sem_inc(gate["pool"], 1)
            pool.tensor_scalar(q.negc[:, :, :], q.adjf_sb[:, :, :], 0.0, MASKED, ALU.is_equal, ALU.mult).then_inc(q.sig["mask"].sem, 1)
            pool.tensor_scalar(q.neg1[:, :, 0:N], q.adjf_sb[:, :, :], 0.0, MASKED_L1, ALU.is_le, ALU.mult).then_inc(q.sig["mask"].sem, 1)
            pool.wait_ge(*q.sig["mask"].at(g, 2))
            pool.sem_inc(gate["pool"], 1)
            pool_spread(pool, q, q.neg1)
            pool.tensor_scalar(q.negm[:, :, 0:N], q.adjf_sb[:, :, :], 0.0, MASKED, ALU.is_equal, ALU.mult).then_inc(q.sig["mask"].sem, 1)
            pool.wait_ge(*q.sig["mask"].at(g, 5))
            pool.sem_inc(gate["pool"], 1)
            pool_spread(pool, q, q.negm)
            yield 0.9
            pool_norm(pool, q, g, 0)

        def l1_tensor(pe, q, g):
            yield 0.0
            pe.wait_ge(*q.sig["z"].at(g, TILES))
            pe_xt(pe, q, g, 1, q.xrow)
            pe.wait_ge(*q.sig["mask"].at(g, 4))
            for t in range(TILES):
                ins = pe.transpose(q.bank[:, 3, t * P:(t + 1) * P], q.neg1[:, t, :], ident[:, :])
            ins.then_inc(q.sig["negt_ps"].sem, 1)
            yield 0.2
            pe.wait_ge(*q.sig["xt_lo"].at(g, 2))
            pe_rows(pe, q, 2, W1H).then_inc(q.sig["wh_ps"].sem, 1)
            pe_rep(pe, q, 0)
            yield 0.7
            pe.wait_ge(*q.sig["e_norm"].at(g, 2))
            pe.wait_ge(*q.sig["wh_sb"].at(g, 1))
            pe_agg(pe, q, 0, q.scores[:, :, :].rearrange("p t j -> p (t j)"), q.val)

        def l1_scalar(act, q, g):
            yield 0.0
            act_xt(act, q, g, 1)
            yield 0.2
            act.wait_ge(*q.sig["wh_ps"].at(g, 1))
            act.activation(q.val[:, :, :].rearrange("p t d -> p (t d)"), q.bank[:, 2, :], ACT.Copy).then_inc(q.sig["wh_sb"].sem, 1)
            act.wait_ge(*q.sig["lin_ps"].at(g, 1))
            act.wait_ge(*q.sig["sc_dot"].at(g, TILES))
            for t in range(TILES):
                act.activation(q.scores[:, t, :], q.bank[:, 1, t * P:(t + 1) * P], ACT.Identity, bias=q.sc[:, t:t + 1]).then_inc(q.sig["lin"].sem, 1)
            yield 0.4
            act_exp(act, q, g, 0)
            yield 0.7
            act.wait_ge(*q.sig["agg_ps"].at(g, 1))
            act.activation(q.u_sb[:, :, :].rearrange("p t d -> p (t d)"), q.bank[:, 0, :], ACT.Copy).then_inc(q.sig["h1_sb"].sem, 1)

        def l1_vector(dve, q, g):
            yield 0.0
            dve_xt(dve, q, g, 1)
            yield 0.2
            dve.wait_ge(*q.sig["wh_sb"].at(g, 1))
            for t in range(TILES):
                dve.tensor_tensor_reduce(out=q.val_sw[:, t, :], in0=q.val[:, t, :], in1=row[:, R_A2, :], scale=1.0, scalar=0.0,
                                         op0=ALU.mult, op1=ALU.add, accum_out=q.sc[:, t:t + 1]).then_inc(q.sig["sc_dot"].sem, 1)
            dve.wait_ge(*q.sig["negt_ps"].at(g, 1))
            dve_leaky(dve, q, g, 0)
            dve_mask_max(dve, q, g, 0, q.scores[:, :, :], q.bank[:, 3, 0:TILES * P].rearrange("p (t j) -> p t j", t=TILES))
            yield 0.4
            dve_inv(dve, q, g, 0)
            dve.wait_ge(*q.sig["e_inv"].at(g, 1))
            for t in range(TILES):
                dve.tensor_scalar(q.scores[:, t, :], q.scores[:, t, :], q.sm[:, t:t + 1], None, ALU.mult).then_inc(q.sig["e_norm"].sem, 1)
            yield 0.7
            dve.wait_ge(*q.sig["h1_sb"].at(g, 1))
            dve.scalar_tensor_tensor(out=q.u_sb[:, :, :], in0=q.u_sb[:, :, :], scalar=0.2, in1=q.u_sb[:, :, :],
                                     op0=ALU.mult, op1=ALU.max).then_inc(q.sig["leaky"].sem, 1)
            dve.wait_ge(*q.sig["leaky"].at(g, 1))
            dve.tensor_tensor(q.u_sb[:, :, :], q.u_sb[:, :, :], q.xrow[:, :, :], ALU.add).then_inc(q.sig["u"].sem, 1)
            dve_norm(dve, q, g, 1, q.xrow)

        def l1_gpsimd(pool, q, g):
            yield 0.7
            pool_norm(pool, q, g, 1)

        def l2_tensor(pe, q, g):
            yield 0.0
            pe.wait_ge(*q.sig["z"].at(g, 2 * TILES))
            pe_xt(pe, q, g, 2, q.xrow)
            yield 0.15
            pe.wait_ge(*q.sig["xt_lo"].at(g, 3))
            pe_cols(pe, q, 1, W2T).then_inc(q.sig["h_ps"].sem, 1)
            pe_cols(pe, q, 2, W2M).then_inc(q.sig["h_ps"].sem, 1)
            yield 0.3
            pe_rows(pe, q, 3, W2T).then_inc(q.sig["h_ps"].sem, 1)
            pe.wait_ge(*q.sig["h_sb"].at(g, 2))
            pe.wait_ge(*q.sig["ha_sb"].at(g, 2))
            for t in range(TILES):
                for k in range(KC):
                    ins = pe.matmul(q.bank[:, 0, t * P:(t + 1) * P], q.work[:, KC + k, t * P:(t + 1) * P], q.work[:, k, t * P:(t + 1) * P],
                                    start=(k == 0), stop=(k == KC - 1))
            ins.then_inc(q.sig["sc_ps"].sem, 1)
            yield 0.5
            pe_pt(pe, q, g, 1, 1)
            yield 0.6
            pe.wait_ge(*q.sig["pt_sb"].at(g, 1))
            pe.wait_ge(*q.sig["hrow_sb"].at(g, 1))
            pe_agg(pe, q, 2, q.pt, q.val)

        def l2_scalar(act, q, g):
            yield 0.0
            act_xt(act, q, g, 2)
            yield 0.15
            act.wait_ge(*q.sig["h_ps"].at(g, 1))
            for o in range(KC):
                act.activation(q.work[:, o, :], q.bank[:, 1, o * R:(o + 1) * R], ACT.Identity, bias=col[:, C_LB + o:C_LB + o + 1]).then_inc(q.sig["h_sb"].sem, 1)
            yield 0.4
            act_exp(act, q, g, 1)
            yield 0.5
            act_pt(act, q, g, 1, 1)
            yield 0.7
            act.wait_ge(*q.sig["elu_m"].at(g, 1))
            m = q.work[:, 0:TILES, :]
            act.activation(m, m, ACT.Exp).then_inc(q.sig["elu_e"].sem, 1)

        def l2_vector(dve, q, g):
            yield 0.0
            dve_xt(dve, q, g, 2)
            yield 0.15
            dve.wait_ge(*q.sig["h_ps"].at(g, 2))
            for o in range(KC):
                dve.tensor_scalar(q.work[:, KC + o, :], q.bank[:, 2, o * R:(o + 1) * R], mcol[:, o:o + 1], None, ALU.add).then_inc(q.sig["ha_sb"].sem, 1)
            yield 0.3
            dve.wait_ge(*q.sig["h_ps"].at(g, 3))
            dve.tensor_tensor(q.val[:, :, :], q.bank[:, 3, :].rearrange("p (t d) -> p t d", t=TILES),
                              row[:, R_LB:R_LB + 1, :].to_broadcast([P, TILES, D]), ALU.add).then_inc(q.sig["hrow_sb"].sem, 1)
            dve.wait_ge(*q.sig["sc_ps"].at(g, 1))
            dve.wait_ge(*q.sig["mask"].at(g, 7))
            dve_mask_max(dve, q, g, 1, q.bank[:, 0, 0:TILES * P].rearrange("p (t j) -> p t j", t=TILES), q.negm[:, :, :])
            yield 0.5
            dve_inv(dve, q, g, 1)
            yield 0.6
            dve.wait_ge(*q.sig["agg_ps"].at(g, 2))
            dve.wait_ge(*q.sig["e_inv"].at(g, 2))
            for t in range(TILES):
                dve.tensor_scalar(q.u_sb[:, t, :], q.bank[:, 2, t * D:(t + 1) * D], q.sm[:, t:t + 1], None, ALU.mult).then_inc(q.sig["elu_y"].sem, 1)
            dve.wait_ge(*q.sig["elu_y"].at(g, 2))
            dve.tensor_scalar(q.work[:, 0:TILES, :], q.u_sb[:, :, :], 0.0, None, ALU.min).then_inc(q.sig["elu_m"].sem, 1)
            yield 0.8
            dve.wait_ge(*q.sig["elu_e"].at(g, 1))
            dve.scalar_tensor_tensor(out=q.u_sb[:, :, :], in0=q.u_sb[:, :, :], scalar=0.0, in1=q.work[:, 0:TILES, :],
                                     op0=ALU.max, op1=ALU.add).then_inc(q.sig["elu_s"].sem, 1)
            dve.wait_ge(*q.sig["elu_s"].at(g, 1))
            dve.scalar_tensor_tensor(out=q.u_sb[:, :, :], in0=q.u_sb[:, :, :], scalar=-1.0, in1=q.xrow[:, :, :],
                                     op0=ALU.add, op1=ALU.add).then_inc(q.sig["u"].sem, 1)
            dve_norm(dve, q, g, 2, q.xkeep)

        def l2_gpsimd(pool, q, g):
            yield 0.5
            pool.wait_ge(*q.sig["e_add"].at(g, 2))
            pool.tensor_tensor(q.adjf_sb[:, :, :], q.adjf_sb[:, :, :], eye[:, :].unsqueeze(1).to_broadcast([P, TILES, N]), ALU.add).then_inc(q.sig["mask"].sem, 1)
            pool.wait_ge(*q.sig["mask"].at(g, 8))
            pool.sem_inc(gate["pool"], 1)
            pool.tensor_scalar(q.negm[:, :, 0:N], q.adjf_sb[:, :, :], 0.0, MASKED, ALU.is_le, ALU.mult).then_inc(q.sig["mask"].sem, 1)
            pool.wait_ge(*q.sig["mask"].at(g, 9))
            pool.sem_inc(gate["pool"], 1)
            pool_spread(pool, q, q.negm)
            yield 0.8
            pool_norm(pool, q, g, 2)

        def at_tensor(pe, q, g, l):
            src = q.xrow if l else q.xkeep
            yield 0.0
            if l:
                pe.wait_ge(*q.sig["aff"].at(g, l))
            else:
                pe.wait_ge(*q.sig["z"].at(g, 3 * TILES))
            pe_xt(pe, q, g, 3 + 2 * l, src)
            yield 0.15
            pe.wait_ge(*q.sig["xt_lo"].at(g, 4 + 2 * l))
            pe_rep(pe, q, 1 + l)
            yield 0.5
            pe_pt(pe, q, g, 2 + l, 2)
            yield 0.65
            pe.wait_ge(*q.sig["pt_sb"].at(g, 2 + l))
            pe_agg(pe, q, 3, q.pt, src)

        def at_scalar(act, q, g, l):
            yield 0.0
            act_xt(act, q, g, 3 + 2 * l)
            yield 0.15
            act.wait_ge(*q.sig["lin_ps"].at(g, 2 + l))
            act.wait_ge(*q.sig["sc_ready"].at(g, 1 + l))
            for t in range(TILES):
                act.activation(q.scores[:, t, :], q.bank[:, 1, t * P:(t + 1) * P], ACT.Identity, bias=q.sc[:, t:t + 1]).then_inc(q.sig["lin"].sem, 1)
            yield 0.35
            act_exp(act, q, g, 2 + l)
            yield 0.5
            act_pt(act, q, g, 2 + l, 2)

        def at_vector(dve, q, g, l):
            src = q.xrow if l else q.xkeep
            yield 0.0
            if l:
                dve.wait_ge(*q.sig["aff"].at(g, l))
            else:
                dve.wait_ge(*q.sig["z"].at(g, 3 * TILES))
            for t in range(TILES):
                dve.tensor_tensor_reduce(out=q.val[:, t, :], in0=src[:, t, :], in1=row[:, R_WI + l, :], scale=1.0, scalar=0.0,
                                         op0=ALU.mult, op1=ALU.add, accum_out=q.sc[:, t:t + 1]).then_inc(q.sig["sc_dot"].sem, 1)
            dve.wait_ge(*q.sig["sc_dot"].at(g, TILES * (2 + l)))
            dve.tensor_scalar(q.sc[:, :], q.sc[:, :], col[:, C_AB + l:C_AB + l + 1], None, ALU.add).then_inc(q.sig["sc_ready"].sem, 1)
            dve_xt(dve, q, g, 3 + 2 * l)
            yield 0.15
            if l == 0:
                dve.wait_ge(*q.sig["mask"].at(g, 11))
            dve_leaky(dve, q, g, 1 + l)
            dve_mask_max(dve, q, g, 2 + l, q.scores[:, :, :], q.negm[:, :, :])
            yield 0.5
            dve_inv(dve, q, g, 2 + l)
            yield 0.65
            dve.wait_ge(*q.sig["agg_ps"].at(g, 3 + l))
            dve.wait_ge(*q.sig["e_inv"].at(g, 3 + l))
            for t in range(TILES):
                ins = dve.scalar_tensor_tensor(out=q.u_sb[:, t, :], in0=q.bank[:, 3, t * D:(t + 1) * D], scalar=q.sm[:, t:t + 1], in1=src[:, t, :],
                                               op0=ALU.mult, op1=ALU.add)
                ins.then_inc(q.sig["u" if t else "u_b"].sem, 1)
            dve.wait_ge(*q.sig["u_b"].at(g, 1 + l))
            dve_norm(dve, q, g, 3 + 2 * l, q.u_sb)

        def at_gpsimd(pool, q, g, l):
            yield 0.65
            pool_norm(pool, q, g, 3 + 2 * l)
            yield 0.9
            pool.wait_ge(*q.sig["z"].at(g, TILES * (4 + 2 * l)))
            pool.tensor_tensor(q.val_sw[:, :, :], q.u_sb[:, :, :], row[:, R_G1 + l:R_G1 + l + 1, :].to_broadcast([P, TILES, D]), ALU.mult).then_inc(q.sig["hb1"].sem, 1)
            pool.wait_ge(*q.sig["hb1"].at(g, 1 + l))
            pool.tensor_tensor(q.val_sw[:, :, :], q.val_sw[:, :, :], row[:, R_B1 + l:R_B1 + l + 1, :].to_broadcast([P, TILES, D]), ALU.add).then_inc(q.sig["hb"].sem, 1)

        def ff_tensor(pe, q, g, l, fn):
            yield 0.0
            pe.wait_ge(*q.sig["z"].at(g, TILES * (4 + 2 * l)))
            pe_xt(pe, q, g, 4 + 2 * l, q.u_sb)
            for f in range(FC + 1):
                yield 0.1 + 0.1 * f
                if f == 0:
                    pe.wait_ge(*q.sig["xt_lo"].at(g, 5 + 2 * l))
                if f < FC:
                    if f >= 2:
                        pe.wait_ge(*ff_act.at(fn, f - 1))
                    for k in range(KC):
                        ins = split3(pe, q.bank[:, 1 + f % 2, 0:R], w1_h[:, l, k, f * P:(f + 1) * P], w1_l[:, l, k, f * P:(f + 1) * P],
                                     q.xt_h[:, k, :], q.xt_l[:, k, :], k == 0, k == KC - 1)
                    ins.then_inc(q.sig["f_ps"].sem, 1)
                if f:
                    c = f - 1
                    pe.wait_ge(*ff_lo.at(fn, c + 1))
                    for t in range(TILES):
                        ins = split3(pe, q.bank[:, 3, t * D:(t + 1) * D], g_hi[:, c % 2, t * P:(t + 1) * P], g_lo[:, c % 2, t * P:(t + 1) * P],
                                     w2_h[:, l, c, :], w2_l[:, l, c, :], c == 0, c == FC - 1, start=(t == 0))
                    ins.then_inc(ff_used.sem, 1)

        def ff_scalar(act, q, g, l, fn):
            yield 0.0
            act_xt(act, q, g, 4 + 2 * l)
            for f in range(FC):
                yield 0.1 + 0.1 * f
                act.wait_ge(*q.sig["f_ps"].at(g, l * FC + f + 1))
                if f >= 4:
                    act.wait_ge(*ff_lo.at(fn, f - 3))
                act.activation(q.work[:, f % 4, :], q.bank[:, 1 + f % 2, 0:R], ACT.Gelu, bias=ffb[:, l * FC + f:l * FC + f + 1]).then_inc(ff_act.sem, 1)

        def ff_vector(dve, q, g, l, fn):
            yield 0.0
            dve_xt(dve, q, g, 4 + 2 * l)
            for f in range(FC):
                yield 0.1 + 0.1 * f
                if not (isinstance(fn, int) and fn == 0 and f < 2):
                    dve.wait_ge(*ff_used.at(fn, f - 1))
                dve.wait_ge(*ff_act.at(fn, f + 1))
                dve.tensor_copy(g_hi[:, f % 2, :], q.work[:, f % 4, :]).then_inc(ff_hi.sem, 1)
                dve.wait_ge(*ff_hi.at(fn, f + 1))
                dve.tensor_tensor(g_lo[:, f % 2, :], q.work[:, f % 4, :], f32(g_hi[:, f % 2, :]), ALU.subtract).then_inc(ff_lo.sem, 1)
            yield 0.9
            dve.wait_ge(*ff_used.at(fn, FC))
            dve.wait_ge(*q.sig["hb"].at(g, 1 + l))
            dve.tensor_tensor(q.u_sb[:, :, :], q.val_sw[:, :, :], q.bank[:, 3, :].rearrange("p (t d) -> p t d", t=TILES), ALU.add).then_inc(q.sig["u"].sem, 1)
            dve_norm(dve, q, g, 4 + 2 * l, q.u_sb)
            dve.wait_ge(*q.sig["z"].at(g, TILES * (5 + 2 * l)))
            dve.tensor_tensor(q.u_sb[:, :, :], q.u_sb[:, :, :], row[:, R_G2 + l:R_G2 + l + 1, :].to_broadcast([P, TILES, D]), ALU.mult).then_inc(q.sig["aff1"].sem, 1)
            dve.wait_ge(*q.sig["aff1"].at(g, 1 + l))
            dve.tensor_tensor(q.xrow[:, :, :], q.u_sb[:, :, :], row[:, R_B2 + l:R_B2 + l + 1, :].to_broadcast([P, TILES, D]), ALU.add).then_inc(q.sig["aff"].sem, 1)
            if l == L - 1:
                dve.wait_ge(*q.sig["aff"].at(g, L))
                dve.tensor_tensor(q.u_sb[:, :, :], q.xrow[:, :, :], q.xkeep[:, :, :], ALU.add).then_inc(q.sig["u"].sem, 1)
                dve_norm(dve, q, g, 9, q.xrow)

        def ff_gpsimd(pool, q, g, l, fn):
            yield 0.9
            pool_norm(pool, q, g, 4 + 2 * l)
            if l == L - 1:
                pool_norm(pool, q, g, 9)

        def sync_out(sp, q, g):
            yield 0.99
            sp.wait_ge(*q.sig["z"].at(g, 10 * TILES))
            sp.sem_inc(gate["sp"], 1)
            sp.dma_start(out_v[2 * g + q.s], q.xrow[:, :, :]).then_inc(q.sig["out"].sem, 16)

        def sync_load(sp, q, g):
            sp.dma_start(q.xin[:, :, :], x_v[2 * g + q.s]).then_inc(q.sig["load"].sem, 16)
            sp.dma_start(q.adji[:, :, :], adj_v[2 * g + q.s]).then_inc(q.sig["load"].sem, 16)

        def phase(eng, kind, ph, q, g, fn, more):
            if kind == "sync":
                if ph == 6 and more:
                    yield 0.0
                    sp = eng
                    sp.wait_ge(*q.sig["u"].at(g, 1))
                    sp.sem_inc(gate["sp"], 1)
                    sp.wait_ge(*q.sig["adjf"].at(g, 1))
                    sp.sem_inc(gate["sp"], 1)
                    sync_load(sp, q, g + 1)
                if ph == PHASES - 1:
                    yield from sync_out(eng, q, g)
                return
            table = {
                "tensor": (l0_tensor, l1_tensor, l2_tensor, at_tensor, ff_tensor),
                "scalar": (l0_scalar, l1_scalar, l2_scalar, at_scalar, ff_scalar),
                "vector": (l0_vector, l1_vector, l2_vector, at_vector, ff_vector),
                "gpsimd": (l0_gpsimd, l1_gpsimd, l2_gpsimd, at_gpsimd, ff_gpsimd),
            }[kind]
            if ph < 3:
                yield from table[ph](eng, q, g)
            elif ph % 2:
                yield from table[3](eng, q, g, (ph - 3) // 2)
            else:
                yield from table[4](eng, q, g, (ph - 4) // 2, fn)

        A, B = streams
        LAG = 6

        def empty():
            return
            yield

        def whole(eng, kind):
            for ph in range(LAG):
                merged(empty(), phase(eng, kind, ph, B, 0, 0, True))

            def period(i, last):
                fn = 1 + i * 2 * L
                for ph in range(PHASES):
                    b = (ph + LAG) % PHASES
                    wraps = ph + LAG >= PHASES
                    a_ff = ph >= 3 and ph % 2 == 0
                    b_ff = b >= 3 and b % 2 == 0 and not (last and wraps)
                    a_gen = phase(eng, kind, ph, A, i, fn, not last)
                    if a_ff:
                        fn = fn + 1
                    b_gen = empty() if last and wraps else phase(eng, kind, b, B, i + 1 if wraps else i, fn, not last)
                    if b_ff:
                        fn = fn + 1
                    merged(a_gen, b_gen)

            with eng.Fori(0, groups - 1) as i:
                period(i, False)
            period(groups - 1, True)

        @block.sync
        def _(sp):
            prep_sync(sp)
            for q in (B, A):
                sync_load(sp, q, 0)
                sp.sem_inc(q.sig["out"].sem, 1)
            whole(sp, "sync")
            for q in (A, B):
                sp.wait_ge(q.sig["out"].sem, 16 * groups + 1)

        @block.gpsimd
        def _(pool):
            prep_gpsimd(pool)
            pool.wait_ge(consts, 1)
            whole(pool, "gpsimd")

        @block.scalar
        def _(act):
            prep_scalar(act)
            act.wait_ge(consts, 1)
            whole(act, "scalar")

        @block.vector
        def _(dve):
            prep_vector(dve)
            dve.wait_ge(consts, 1)
            whole(dve, "vector")

        @block.tensor
        def _(pe):
            prep_tensor(pe)
            pe.wait_ge(consts, 1)
            pe.wait_ge(ident_ready, 3)
            whole(pe, "tensor")


_SMALL = (("L0_gnn_Wq", "L0_gnn_Wk"), ("L0_gnn_Wv", "L0_gnn_Wo"), ("L1_gnn_W", "L2_gnn_W^T"), ("L2_gnn_W", "L2_gnn_attn"))


def kernel(**inputs):
    import numpy as np
    import concourse.bacc as bacc
    from concourse.bass_utils import run_bass_kernel_spmd as run

    a = {k: np.asarray(v) for k, v in inputs.items()}
    x = a["x"]
    B, n, d = x.shape

    def by_partition(v):
        return v.reshape(-1, P).T

    get = lambda name: a[name[:-2]].T if name.endswith("^T") else a[name]
    w = a["L3_gnn_attn_w"]
    cols = np.concatenate([
        by_partition(a["L3_gnn_b1"]), by_partition(a["L3_gnn_beta1"]), by_partition(a["L3_gnn_g1"]),
        by_partition(w[:, d:]), by_partition(a["L2_gnn_b"]), np.broadcast_to(a["L3_gnn_attn_b"], (P, L))], axis=1)
    rows = np.concatenate([
        w[:, :d], a["L3_gnn_g1"], a["L3_gnn_beta1"], a["L3_gnn_g2"], a["L3_gnn_beta2"],
        a["L1_gnn_a"][d:].reshape(1, d), a["L2_gnn_b"].reshape(1, d)], axis=0)
    prep_rows = np.concatenate([a["L1_gnn_a"][:d].reshape(1, d), a["L3_gnn_b2"]], axis=0)
    arrays = {
        "x_in": x.reshape(B * n, d),
        "adj_in": a["adj"].reshape(B * n, n),
        "w_small": np.stack([np.concatenate([get(u), get(v)], axis=0) for u, v in _SMALL]),
        "w1": a["L3_gnn_W1"],
        "w2": a["L3_gnn_W2"],
        "cols": cols,
        "rows": rows,
        "prep_rows": prep_rows,
    }
    arrays = {k: np.ascontiguousarray(v) for k, v in arrays.items()}
    nc = bacc.Bacc("TRN2", target_bir_lowering=False, num_devices=1)
    args = [nc.dram_tensor(k, v.shape, mybir.dt.from_np(v.dtype), kind="ExternalInput").ap() for k, v in arrays.items()]
    out = nc.dram_tensor("out", (B * n, d), F32, kind="ExternalOutput").ap()
    gnn_kernel(nc, *args, out)
    r = run(nc, [arrays], core_ids=[0])
    return r.results[0]["out"].reshape(B, n, d)
```

```python
from contextlib import ExitStack

import concourse.bass as bass
from concourse import mybir

F32 = mybir.dt.float32
F32R = mybir.dt.float32r
I32 = mybir.dt.int32
ALU = mybir.AluOpType
ACT = mybir.ActivationFunctionType
AX_X = mybir.AxisListType.X

P = 128
D = 256
KC = D // P
N = 64
TILES = 2
R = TILES * P
NH = 8
DK = D // NH
RG = 4
HC = NH // RG
L = 3
FF = 4 * D
FC = FF // P
EPS = 1e-5
MASKED = -1e30
OTHER = -3e38
MASKED_L1 = -9e15
WQ, WK, WV, WO, W1H, W2T, W2M = range(7)
R_WI, R_G1, R_B1, R_G2, R_B2, R_A2, R_LB = 0, L, 2 * L, 3 * L, 4 * L, 5 * L, 5 * L + 1
ROWS = 5 * L + 2
PHASES = 9


class Stream:
    pass


class Signal:

    def __init__(self, sem, per):
        self.sem, self.per = sem, per

    def at(self, g, k):
        return self.sem, g * self.per + k


def merged(a, b):
    pa, pb = next(a, None), next(b, None)
    while pa is not None or pb is not None:
        if pb is None or (pa is not None and pa <= pb):
            pa = next(a, None)
        else:
            pb = next(b, None)


def gnn_kernel(nc, x, adj, w_small, w1, w2, cols, rows, prep_rows, out):
    groups = x.shape[0] // (2 * R)
    x_v = x.rearrange("(n t p) d -> n p t d", t=TILES, p=P)
    out_v = out.rearrange("(n t p) d -> n p t d", t=TILES, p=P)
    adj_v = adj.rearrange("(n t p) j -> n p t j", t=TILES, p=P)
    C_FB, C_BETA1, C_G1, C_WJ, C_LB, C_AB, C_G2 = 0, L * FC, L * FC + L * KC, L * FC + 2 * L * KC, L * FC + 3 * L * KC, L * FC + 3 * L * KC + KC, L * FC + 3 * L * KC + KC + L
    NCOLS = C_G2 + L * KC

    with ExitStack() as ctx:
        def sb(name, shape, dt=F32):
            return ctx.enter_context(nc.sbuf_tensor(name, shape, dt))

        def sem(name):
            return ctx.enter_context(nc.semaphore(name))

        ws_h = sb("ws_h", [P, 7, KC, D], F32R)
        ws_l = sb("ws_l", [P, 7, KC, D], F32R)
        w1_h = sb("w1_h", [P, L, KC, FF], F32R)
        w1_l = sb("w1_l", [P, L, KC, FF], F32R)
        w2_h = sb("w2_h", [P, L, FC, D], F32R)
        w2_l = sb("w2_l", [P, L, FC, D], F32R)
        rep_h = sb("rep_h", [P, 1 + L, KC, P], F32R)
        rep_l = sb("rep_l", [P, 1 + L, KC, P], F32R)
        col = sb("col", [P, NCOLS])
        row = sb("row", [P, ROWS, D])
        ident = sb("ident", [P, P])
        eye = sb("eye", [P, N])
        ffb = sb("ffb", [P, L * FC])
        mcol = sb("mcol", [P, KC])
        wa1 = sb("wa1", [P, KC])
        other = sb("other", [P, 2])
        abias = sb("abias", [P, L])
        mhalf = sb("mhalf", [P, TILES])

        w_in = [sem(f"w_in{i}") for i in range(2)]
        c_in = sem("c_in")
        ones_ready = sem("ones_ready")
        ident_ready = sem("ident_ready")
        w_hi = sem("w_hi")
        w_lo = sem("w_lo")
        w_used = sem("w_used")
        prep_dve = sem("prep_dve")
        prep_act = sem("prep_act")
        prep_pe = sem("prep_pe")
        consts = sem("consts")
        gate = {name: sem(f"gate_{name}") for name in ("pe", "dve", "pool", "sp")}
        streams = []
        for s in range(2):
            q = Stream()
            q.sig = {name: Signal(sem(f"{name}_{s}"), per) for name, per in dict(
                load=32, out=16, adjf=1, mask=11,
                xt_ps=18, xt_hi=18, xt_lo=18,
                qkv_ps=3, qk_sb=2, v_sb=1, vsw_sb=2,
                s_ps=1, p_add=2, p_max=2, p_sub=2, p_exp=2, p_div=4, p_norm=2,
                pt0_ps=2, pt0_sb=2, pv0_ps=2, o_hi=2, o_lo=2, y_ps=1,
                negt_ps=1, lin_ps=4, wh_ps=1, wh_sb=1, sc_dot=8, sc_ready=3, lin=8,
                h_ps=3, h_sb=2, ha_sb=2, hrow_sb=1, sc_ps=1,
                e_add=5, e_max=5, e_exp=10, e_inv=5, e_norm=2,
                pt_ps=4, pt_sb=4, agg_ps=10, leaky=1, h1_sb=1, leak=4, elu=3, elu_m=1, elu_e=1,
                u=10, st=20, mv=20, ve=10, rstd=10, z=20,
                hb=6, f_ps=24, ff_gelu=24, ff_hi=24, ff_lo=24, ff_used=24, u_b=3, aff=6,
            ).items()}
            q.s = s
            q.xin = sb(f"xin{s}", [P, TILES, D])
            q.xrow = sb(f"xrow{s}", [P, TILES, D])
            q.u_sb = sb(f"u{s}", [P, TILES, D])
            q.xkeep = sb(f"xkeep{s}", [P, TILES, D])
            q.xt_h = sb(f"xt_h{s}", [P, KC, R], F32R)
            q.xt_l = sb(f"xt_l{s}", [P, KC, R], F32R)
            q.val = sb(f"val{s}", [P, TILES, D])
            q.val_sw = sb(f"val_sw{s}", [P, TILES, D])
            q.work = sb(f"work{s}", [P, 4, R])
            q.pt = sb(f"pt{s}", [P, 4 * P])
            q.adji = sb(f"adji{s}", [P, TILES, N], I32)
            q.adjf_sb = sb(f"adjf{s}", [P, TILES, N])
            q.negc = sb(f"negc{s}", [P, TILES, N])
            q.neg1 = q.u_sb[:, :, 0:P]
            q.g_hi = sb(f"g_hi{s}", [P, 2, R], F32R)
            q.g_lo = sb(f"g_lo{s}", [P, 2, R], F32R)
            q.negm = sb(f"negm{s}", [P, TILES, P])
            q.mx = sb(f"mx{s}", [P, NH * TILES])
            q.sm = sb(f"sm{s}", [P, NH * TILES])
            q.stat = sb(f"stat{s}", [P, TILES, 6])
            q.mv_sb = sb(f"mv{s}", [P, TILES, 2])
            q.ve_sb = sb(f"ve{s}", [P, TILES])
            q.rstd_sb = sb(f"rstd{s}", [P, TILES])
            q.sc = sb(f"sc{s}", [P, TILES])
            q.bank = ctx.enter_context(nc.psum_tensor(f"bank{s}", [P, 4, 512], F32))
            q.scores = q.pt[:, 2 * P:].rearrange("p (t j) -> p t j", t=TILES)
            streams.append(q)

        def f32(ap):
            return ap.bitcast(F32)

        def split3(pe, out_ap, lh, ll, rh, rl, first, last, start=True):
            pe.matmul(out_ap, lh, rh, start=first and start, stop=False, skip_group_check=True)
            pe.matmul(out_ap, lh, rl, start=False, stop=False, skip_group_check=True)
            return pe.matmul(out_ap, ll, rh, start=False, stop=last, skip_group_check=True)

        stage = [streams[u].work[:].rearrange("p a b -> p (a b)") for u in range(2)]
        units = [("small", i) for i in range(3)] + [("mix", 0)] + [("w1", l, k) for l in range(L) for k in range(KC)] \
            + [("w2", l, h) for l in range(L) for h in range(2)]

        block = ctx.enter_context(nc.Block())

        def unit_src(u):
            if u[0] in ("small", "mix"):
                i = u[1] if u[0] == "small" else 3
                return w_small[i].rearrange("(m k p) n -> p m k n", m=2, p=P), "p (m k n) -> p m k n", dict(m=2, k=KC)
            if u[0] == "w1":
                return w1[u[1], u[2] * P:(u[2] + 1) * P, :], None, None
            return w2[u[1], u[2] * 512:(u[2] + 1) * 512, :].rearrange("(f p) d -> p f d", p=P), "p (f d) -> p f d", dict(f=4)

        def unit_dst(u, part):
            ws, wa, wb = (ws_h, w1_h, w2_h) if part == "hi" else (ws_l, w1_l, w2_l)
            if u[0] == "small":
                return ws[:, 2 * u[1]:2 * u[1] + 2, :, :].rearrange("p m k n -> p (m k n)")
            if u[0] == "w1":
                return wa[:, u[1], u[2], :]
            return wb[:, u[1], 4 * u[2]:4 * u[2] + 4, :].rearrange("p f d -> p (f d)")

        def prep_sync(sp):
            sp.dma_start(col[:, :], cols).then_inc(c_in, 16)
            sp.dma_start(row[:, :, :], rows.partition_broadcast(P)).then_inc(c_in, 16)
            sp.dma_start(streams[0].xrow[:, 0, :], prep_rows[0].partition_broadcast(P)).then_inc(c_in, 16)
            sp.dma_start(streams[0].val[:, :, :], prep_rows[1:3].partition_broadcast(P)).then_inc(c_in, 16)
            sp.dma_start(streams[0].val_sw[:, 0, :], prep_rows[3].partition_broadcast(P)).then_inc(c_in, 16)
            sp.dma_start(streams[0].xkeep[:, :, :], prep_rows[4:4 + L - 1].partition_broadcast(P)).then_inc(c_in, 16)
            for i, u in enumerate(units):
                src, pat, kw = unit_src(u)
                if i >= 2:
                    sp.wait_ge(w_lo, i - 1)
                    if 3 <= i - 2 < 4 + L * KC:
                        sp.wait_ge(w_used, i - 4)
                dst = stage[i % 2] if pat is None else stage[i % 2].rearrange(pat, **kw)
                sp.dma_start(dst, src).then_inc(w_in[i % 2], 16)

        def prep_scalar(act):
            act.wait_ge(c_in, 96)
            for i, u in enumerate(units):
                act.wait_ge(w_in[i % 2], 16 * (i // 2 + 1))
                if u[0] == "mix":
                    act.wait_ge(prep_pe, 1)
                    act.activation(ws_h[:, W2M, :, :].rearrange("p k n -> p (k n)"), streams[0].bank[:, 0, :], ACT.Copy).then_inc(w_hi, 1)
                elif u[0] == "w1":
                    c = C_G1 + u[1] * KC + u[2]
                    act.activation(unit_dst(u, "hi"), stage[i % 2], ACT.Copy, scale=col[:, c:c + 1]).then_inc(w_hi, 1)
                else:
                    act.activation(unit_dst(u, "hi"), stage[i % 2], ACT.Copy).then_inc(w_hi, 1)

        def prep_vector(dve):
            dve.wait_ge(c_in, 96)
            n = 0
            for b in range(2):
                dve.memset(other[b * N:(b + 1) * N, b:b + 1], 0.0).then_inc(prep_dve, 1)
                dve.memset(other[b * N:(b + 1) * N, 1 - b:2 - b], OTHER).then_inc(prep_dve, 1)
                n += 2
            dve.memset(mhalf[:, :], -0.5).then_inc(prep_dve, 1)
            ones = streams[0].pt[:, 0:P]
            dve.memset(ones, 1.0).then_inc(prep_dve, 1)
            n += 2
            dve.tensor_tensor(row[:, R_B1:R_B1 + 2, :], row[:, R_B1:R_B1 + 2, :], streams[0].val[:, :, :], ALU.add).then_inc(prep_dve, 1)
            dve.tensor_tensor(row[:, R_B1 + 2, :], row[:, R_B1 + 2, :], streams[0].val_sw[:, 0, :], ALU.add).then_inc(prep_dve, 1)
            n += 2
            dve.tensor_copy(abias[:, :], col[:, C_AB:C_AB + L]).then_inc(prep_dve, 1)
            n += 1
            for l in range(1, L):
                for part in (streams[0].xkeep[:, l - 1, :], row[:, R_WI + l, :]):
                    dve.wait_ge(prep_dve, n)
                    dve.tensor_tensor_reduce(out=streams[0].u_sb[:, 0, :], in0=part, in1=row[:, R_B2 + l - 1, :], scale=1.0, scalar=abias[:, l:l + 1],
                                             op0=ALU.mult, op1=ALU.add, accum_out=abias[:, l:l + 1]).then_inc(prep_dve, 1)
                    n += 1
                dve.wait_ge(prep_dve, n)
                dve.tensor_tensor(row[:, R_WI + l, :], row[:, R_WI + l, :], row[:, R_G2 + l - 1, :], ALU.mult).then_inc(prep_dve, 1)
                n += 1
            for k in range(KC, L * KC):
                dve.tensor_tensor(col[:, C_WJ + k:C_WJ + k + 1], col[:, C_WJ + k:C_WJ + k + 1], col[:, C_G2 + k - KC:C_G2 + k - KC + 1], ALU.mult).then_inc(prep_dve, 1)
                n += 1
            for i, u in enumerate(units):
                raw = stage[i % 2]
                dve.wait_ge(w_in[i % 2], 16 * (i // 2 + 1))
                dve.wait_ge(w_hi, i + 1)
                if u == ("small", 2):
                    for k in range(KC):
                        dve.wait_ge(prep_dve, n)
                        dve.tensor_tensor_reduce(out=streams[0].u_sb[:, 0, :], in0=raw[:, k * D:(k + 1) * D], in1=streams[0].xrow[:, 0, :],
                                                 scale=1.0, scalar=0.0, op0=ALU.mult, op1=ALU.add,
                                                 accum_out=wa1[:, k:k + 1]).then_inc(prep_dve, 1)
                        n += 1
                if u[0] == "mix":
                    dve.tensor_tensor(ws_l[:, W2M, :, :].rearrange("p k n -> p (k n)"), streams[0].bank[:, 0, :],
                                      f32(ws_h[:, W2M, :, :]).rearrange("p k n -> p (k n)"), ALU.subtract).then_inc(w_lo, 1)
                elif u[0] == "w1":
                    c = C_G1 + u[1] * KC + u[2]
                    dve.scalar_tensor_tensor(out=unit_dst(u, "lo"), in0=raw, scalar=col[:, c:c + 1], in1=f32(unit_dst(u, "hi")),
                                             op0=ALU.mult, op1=ALU.subtract).then_inc(w_lo, 1)
                else:
                    dve.tensor_tensor(unit_dst(u, "lo"), raw, f32(unit_dst(u, "hi")), ALU.subtract).then_inc(w_lo, 1)
            dve.wait_ge(prep_dve, n)
            for m in range(1 + L):
                for k in range(KC):
                    c = wa1[:, k:k + 1] if m == 0 else col[:, C_WJ + (m - 1) * KC + k:C_WJ + (m - 1) * KC + k + 1]
                    dve.tensor_scalar(rep_h[:, m, k, :], ones, c, None, ALU.mult).then_inc(prep_dve, 1)
                    n += 1
                    dve.wait_ge(prep_dve, n)
                    dve.scalar_tensor_tensor(out=rep_l[:, m, k, :], in0=ones, scalar=c, in1=f32(rep_h[:, m, k, :]),
                                             op0=ALU.mult, op1=ALU.subtract).then_inc(prep_dve, 1)
                    n += 1
            dve.wait_ge(w_used, 1)
            dve.tensor_copy(mcol[:, :], streams[0].bank[:, 1, 0:KC]).then_inc(prep_dve, 1)
            dve.wait_ge(w_used, 1 + L * KC)
            dve.tensor_tensor(ffb[:, :], streams[1].bank[:, 0, 0:L * FC], col[:, C_FB:C_FB + L * FC], ALU.add).then_inc(prep_dve, 1)
            n += 2
            dve.wait_ge(prep_dve, n)
            dve.engine_nop().then_inc(consts, 1)

        def prep_tensor(pe):
            pe.wait_ge(c_in, 96)
            for i, u in enumerate(units):
                raw = stage[i % 2]
                pe.wait_ge(w_in[i % 2], 16 * (i // 2 + 1))
                if u[0] == "mix":
                    m = raw.rearrange("p (m k n) -> p m k n", m=2, k=KC)
                    for i2 in range(KC):
                        for o in range(KC):
                            ins = pe.matmul(streams[0].bank[:, 0, i2 * D:(i2 + 1) * D], m[:, 0, o, i2 * P:(i2 + 1) * P], m[:, 1, o, :],
                                            start=(o == 0), stop=(o == KC - 1))
                    ins.then_inc(prep_pe, 1)
                    for j in range(KC):
                        for o in range(KC):
                            ins = pe.matmul(streams[0].bank[:, 1, j:j + 1], m[:, 1, o, j * P:(j + 1) * P], col[:, C_LB + o:C_LB + o + 1],
                                            start=(o == 0), stop=(o == KC - 1))
                    ins.then_inc(w_used, 1)
                elif u[0] == "w1":
                    _, l, k = u
                    for f in range(FC):
                        ins = pe.matmul(streams[1].bank[:, 0, l * FC + f:l * FC + f + 1], raw[:, f * P:(f + 1) * P],
                                        col[:, C_BETA1 + l * KC + k:C_BETA1 + l * KC + k + 1],
                                        start=(l == 0 and k == 0 and f == 0), stop=(k == KC - 1), skip_group_check=True)
                    ins.then_inc(w_used, 1)

        def prep_gpsimd(pool):
            pool.memset(ident[:, :], 0.0).then_inc(ones_ready, 1)
            pool.memset(eye[:, :], 0.0).then_inc(ones_ready, 1)
            pool.wait_ge(ones_ready, 2)
            pool.affine_select(out=ident[:, :], in_=ident[:, :], compare_op=ALU.not_equal, fill=1.0, base=0,
                               pattern=[[-1, P]], channel_multiplier=1).then_inc(ident_ready, 1)
            pool.affine_select(out=eye[:, :], in_=eye[:, :], compare_op=ALU.not_equal, fill=1.0, base=0,
                               pattern=[[-1, N]], channel_multiplier=1).then_inc(ident_ready, 1)
            pool.wait_ge(ident_ready, 2)
            pool.affine_select(out=eye[:, :], in_=eye[:, :], compare_op=ALU.not_equal, fill=1.0, base=-N,
                               pattern=[[-1, N]], channel_multiplier=1).then_inc(ident_ready, 1)
            pool.wait_ge(ident_ready, 3)

        XT = (0, 3)

        def pe_xt(pe, q, g, n, src):
            for k in range(KC):
                for t in range(TILES):
                    ins = pe.transpose(q.bank[:, XT[k], t * P:(t + 1) * P], src[:, t, k * P:(k + 1) * P], ident[:, :])
                ins.then_inc(q.sig["xt_ps"].sem, 1)

        def act_xt(act, q, g, n):
            for k in range(KC):
                yield 0.5 + 0.5 * k
                act.wait_ge(*q.sig["xt_ps"].at(g, KC * n + k + 1))
                act.activation(q.xt_h[:, k, :], q.bank[:, XT[k], 0:R], ACT.Copy).then_inc(q.sig["xt_hi"].sem, 1)

        def dve_xt(dve, q, g, n):
            for k in range(KC):
                yield 1.0 + 0.5 * k
                dve.wait_ge(*q.sig["xt_hi"].at(g, KC * n + k + 1))
                dve.tensor_tensor(q.xt_l[:, k, :], q.bank[:, XT[k], 0:R], f32(q.xt_h[:, k, :]), ALU.subtract).then_inc(q.sig["xt_lo"].sem, 1)

        def pe_wait_xt(pe, q, g, n):
            pe.wait_ge(*q.sig["xt_lo"].at(g, KC * (n + 1)))

        def pe_rows(pe, q, bank, w, done=None):
            for t in range(TILES):
                for k in range(KC):
                    ins = split3(pe, q.bank[:, bank, t * D:(t + 1) * D], q.xt_h[:, k, t * P:(t + 1) * P], q.xt_l[:, k, t * P:(t + 1) * P],
                                 ws_h[:, w, k, :], ws_l[:, w, k, :], k == 0, k == KC - 1)
            return ins

        def pe_cols(pe, q, bank, w):
            for o in range(KC):
                for k in range(KC):
                    ins = split3(pe, q.bank[:, bank, o * R:(o + 1) * R], ws_h[:, w, k, o * P:(o + 1) * P], ws_l[:, w, k, o * P:(o + 1) * P],
                                 q.xt_h[:, k, :], q.xt_l[:, k, :], k == 0, k == KC - 1)
            return ins

        def pe_rep(pe, q, m):
            for k in range(KC):
                ins = split3(pe, q.bank[:, 1, 0:R], rep_h[:, m, k, :], rep_l[:, m, k, :], q.xt_h[:, k, :], q.xt_l[:, k, :], k == 0, k == KC - 1)
            ins.then_inc(q.sig["lin_ps"].sem, 1)

        def dve_norm(dve, q, g, n, at, dst):
            dve.wait_ge(*q.sig["u"].at(g, n + 1))
            for t in range(TILES):
                dve.bn_stats(q.stat[:, t, :], q.u_sb[:, t, :]).then_inc(q.sig["st"].sem, 1)
            yield at + 0.8
            for t in range(TILES):
                dve.wait_ge(*q.sig["st"].at(g, TILES * n + t + 1))
                dve.sem_inc(gate["dve"], 1)
                dve.bn_aggr(q.mv_sb[:, t, :], q.stat[:, t, :]).then_inc(q.sig["mv"].sem, 1)
            dve.wait_ge(*q.sig["mv"].at(g, TILES * (n + 1)))
            dve.tensor_scalar(q.ve_sb[:, :], q.mv_sb[:, :, 1], EPS, None, ALU.add).then_inc(q.sig["ve"].sem, 1)
            yield at + 2.0
            dve.wait_ge(*q.sig["rstd"].at(g, n + 1))
            for t in range(TILES):
                dve.tensor_scalar(dst[:, t, :], q.u_sb[:, t, :], q.mv_sb[:, t, 0:1], q.rstd_sb[:, t:t + 1],
                                  ALU.subtract, ALU.mult).then_inc(q.sig["z"].sem, 1)

        def pool_norm(pool, q, g, n, at):
            yield at + 1.0
            pool.wait_ge(*q.sig["ve"].at(g, n + 1))
            pool.tensor_tensor(q.rstd_sb[:, :], q.ve_sb[:, :], mhalf[:, :], ALU.pow).then_inc(q.sig["rstd"].sem, 1)

        def pool_affine(pool, q, g, l, dst, gain, bias, done):
            pool.tensor_tensor(dst[:, :, :], q.u_sb[:, :, :], row[:, gain + l:gain + l + 1, :].to_broadcast([P, TILES, D]), ALU.mult).then_inc(q.sig[done].sem, 1)
            pool.wait_ge(*q.sig[done].at(g, 2 * l + 1))
            pool.tensor_tensor(dst[:, :, :], dst[:, :, :], row[:, bias + l:bias + l + 1, :].to_broadcast([P, TILES, D]), ALU.add).then_inc(q.sig[done].sem, 1)

        def dve_leaky(dve, q, g, n, at):
            yield at
            dve.wait_ge(*q.sig["lin"].at(g, TILES * (n + 1)))
            dve.scalar_tensor_tensor(out=q.scores[:, :, :], in0=q.scores[:, :, :], scalar=0.2, in1=q.scores[:, :, :],
                                     op0=ALU.mult, op1=ALU.max).then_inc(q.sig["leak"].sem, 1)
            yield at + 0.4
            dve.wait_ge(*q.sig["leak"].at(g, n + 1))

        def dve_mask_max(dve, q, g, n, at, scores, neg):
            dve.tensor_tensor(q.scores[:, :, :], scores, neg, ALU.add).then_inc(q.sig["e_add"].sem, 1)
            yield at
            dve.wait_ge(*q.sig["e_add"].at(g, n + 1))
            dve.tensor_reduce(q.mx[:, 0:TILES], q.scores[:, :, :], AX_X, ALU.max, negate=True).then_inc(q.sig["e_max"].sem, 1)

        def act_exp(act, q, g, n):
            act.wait_ge(*q.sig["e_max"].at(g, n + 1))
            for t in range(TILES):
                act.activation(q.scores[:, t, :], q.scores[:, t, :], ACT.Exp, bias=q.mx[:, t:t + 1],
                               accum_out=q.sm[:, t:t + 1]).then_inc(q.sig["e_exp"].sem, 1)

        def dve_inv(dve, q, g, n):
            dve.wait_ge(*q.sig["e_exp"].at(g, TILES * (n + 1)))
            dve.reciprocal(q.sm[:, 0:TILES], q.sm[:, 0:TILES]).then_inc(q.sig["e_inv"].sem, 1)

        def pe_pt(pe, q, g, n, bank):
            for t in range(TILES):
                pe.wait_ge(*q.sig["e_exp"].at(g, TILES * n + t + 1))
                ins = pe.transpose(q.bank[:, bank, t * P:(t + 1) * P], q.scores[:, t, :], ident[:, :])
            ins.then_inc(q.sig["pt_ps"].sem, 1)

        def act_pt(act, q, g, n, bank):
            act.wait_ge(*q.sig["pt_ps"].at(g, n))
            act.activation(q.pt[:, 0:TILES * P], q.bank[:, bank, 0:TILES * P], ACT.Copy).then_inc(q.sig["pt_sb"].sem, 1)

        def pe_agg(pe, q, banks, lhs, rhs):
            for t in range(TILES):
                pe.matmul(q.bank[:, banks[t], t * D:(t + 1) * D], lhs[:, t * P:(t + 1) * P], rhs[:, t, :], start=True, stop=True).then_inc(q.sig["agg_ps"].sem, 1)

        def l0_tensor(pe, q, g):
            yield 0.0
            pe.wait_ge(*q.sig["load"].at(g, 32))
            pe_xt(pe, q, g, 0, q.xin)
            yield 2.0
            pe_wait_xt(pe, q, g, 0)
            pe_rows(pe, q, 3, WV).then_inc(q.sig["qkv_ps"].sem, 1)
            yield 3.3
            pe_cols(pe, q, 1, WQ).then_inc(q.sig["qkv_ps"].sem, 1)
            yield 4.6
            pe_cols(pe, q, 2, WK).then_inc(q.sig["qkv_ps"].sem, 1)
            yield 6.6
            pe.wait_ge(*q.sig["qk_sb"].at(g, 2))
            pe.wait_ge(*q.sig["vsw_sb"].at(g, 2))
            for t in range(TILES):
                if t:
                    yield 8.2
                for hc in range(HC):
                    for b in range(2):
                        for r in range(RG):
                            c = (t * HC + hc) * N
                            rows_ = slice(t * P + b * N, t * P + (b + 1) * N)
                            ins = pe.matmul(q.bank[b * N:(b + 1) * N, r, c:c + N], q.work[r * DK:(r + 1) * DK, hc, rows_],
                                            q.work[r * DK:(r + 1) * DK, HC + hc, rows_], start=True, stop=True)
            ins.then_inc(q.sig["s_ps"].sem, 1)
            for t in range(TILES):
                yield 14.8 + 1.6 * t
                pe.wait_ge(*q.sig["p_norm"].at(g, t + 1))
                pe.wait_ge(*q.sig["p_add"].at(g, 2))
                for r in range(RG):
                    ins = pe.transpose(q.bank[:, t, r * P:(r + 1) * P], q.work[:, 2 * t + r // 2, (r % 2) * P:(r % 2 + 1) * P], ident[:, :])
                ins.then_inc(q.sig["pt0_ps"].sem, 1)
                yield 16.2 + 1.8 * t
                pe.wait_ge(*q.sig["pt0_sb"].at(g, t + 1))
                pe.sem_inc(gate["pe"], 1)
                for r in range(RG):
                    for b in range(2):
                        for hc in range(HC):
                            v = q.val if b == hc else q.val_sw
                            h = hc * RG + r
                            ins = pe.matmul(q.bank[r * DK:(r + 1) * DK, 2 + hc, t * P + b * N:t * P + (b + 1) * N],
                                            v[hc * N:(hc + 1) * N, t, h * DK:(h + 1) * DK],
                                            q.pt[hc * N:(hc + 1) * N, r * P + b * N:r * P + (b + 1) * N], start=True, stop=True)
                ins.then_inc(q.sig["pv0_ps"].sem, 1)
            yield 20.8
            pe.wait_ge(*q.sig["o_lo"].at(g, 2))
            pe_rows(pe, q, 0, WO).then_inc(q.sig["y_ps"].sem, 1)

        def l0_scalar(act, q, g):
            yield from act_xt(act, q, g, 0)
            yield 3.4
            act.wait_ge(*q.sig["qkv_ps"].at(g, 1))
            act.activation(q.val[:, :, :].rearrange("p t d -> p (t d)"), q.bank[:, 3, :], ACT.Copy).then_inc(q.sig["v_sb"].sem, 1)
            yield 4.7
            act.wait_ge(*q.sig["qkv_ps"].at(g, 2))
            act.activation(q.work[:, 0:HC, :].rearrange("p c r -> p (c r)"), q.bank[:, 1, :], ACT.Copy, scale=DK ** -0.5).then_inc(q.sig["qk_sb"].sem, 1)
            yield 5.9
            act.wait_ge(*q.sig["qkv_ps"].at(g, 3))
            act.activation(q.work[:, HC:2 * HC, :].rearrange("p c r -> p (c r)"), q.bank[:, 2, :], ACT.Copy).then_inc(q.sig["qk_sb"].sem, 1)
            yield 11.9
            act.wait_ge(*q.sig["p_sub"].at(g, 1))
            p = q.work[:, 0:2, :].rearrange("p c r -> p (c r)")
            act.activation(p, p, ACT.Exp).then_inc(q.sig["p_exp"].sem, 1)
            yield 13.9
            act.wait_ge(*q.sig["p_sub"].at(g, 2))
            p = q.work[:, 2:4, :].rearrange("p c r -> p (c r)")
            act.activation(p, p, ACT.Exp).then_inc(q.sig["p_exp"].sem, 1)
            for t in range(TILES):
                yield 15.6 + 1.8 * t
                act.wait_ge(*q.sig["pt0_ps"].at(g, t + 1))
                if t:
                    act.wait_ge(*q.sig["pv0_ps"].at(g, t))
                act.activation(q.pt[:, :], q.bank[:, t, :], ACT.Copy).then_inc(q.sig["pt0_sb"].sem, 1)
            for k in range(KC):
                yield 19.6 + 0.4 * k
                act.wait_ge(*q.sig["pv0_ps"].at(g, 2))
                act.activation(q.xt_h[:, k, :], q.bank[:, 2 + k, 0:R], ACT.Relu).then_inc(q.sig["o_hi"].sem, 1)

        def l0_vector(dve, q, g):
            yield from dve_xt(dve, q, g, 0)
            yield 4.0
            dve.wait_ge(*q.sig["qkv_ps"].at(g, 1))
            dve.wait_ge(*q.sig["v_sb"].at(g, 1))
            for b in range(2):
                dve.tensor_copy(q.val_sw[(1 - b) * N:(2 - b) * N, :, :].rearrange("p t d -> p (t d)"), q.bank[b * N:(b + 1) * N, 3, :]).then_inc(q.sig["vsw_sb"].sem, 1)

            def softmax_front(t, at):
                yield at
                dve.wait_ge(*q.sig["s_ps"].at(g, 1))
                dve.wait_ge(*q.sig["mask"].at(g, 1))
                p4 = q.work[:, 2 * t:2 * t + 2, :].rearrange("p c (r h j) -> p (c r) h j", r=2, h=HC)
                p = q.work[:, 2 * t:2 * t + 2, :].rearrange("p c (h j) -> p (c h) j", j=N)
                m = q.mx[:, t * NH:(t + 1) * NH]
                dve.tensor_tensor(p4, q.bank[:, :, t * HC * N:(t + 1) * HC * N].rearrange("p r (h j) -> p r h j", h=HC),
                                  q.negc[:, t:t + 1, :].unsqueeze(1).to_broadcast([P, RG, HC, N]), ALU.add).then_inc(q.sig["p_add"].sem, 1)
                yield at + 0.7
                dve.wait_ge(*q.sig["p_add"].at(g, t + 1))
                dve.tensor_reduce(m, p, AX_X, ALU.max).then_inc(q.sig["p_max"].sem, 1)
                yield at + 1.3
                dve.wait_ge(*q.sig["p_max"].at(g, t + 1))
                dve.tensor_tensor(p, p, m.unsqueeze(2).to_broadcast([P, NH, N]), ALU.subtract).then_inc(q.sig["p_sub"].sem, 1)

            def softmax_back(t, at):
                yield at
                p = q.work[:, 2 * t:2 * t + 2, :].rearrange("p c (h j) -> p (c h) j", j=N)
                sm = q.sm[:, t * NH:(t + 1) * NH]
                dve.wait_ge(*q.sig["p_exp"].at(g, t + 1))
                dve.tensor_reduce(sm, p, AX_X, ALU.add).then_inc(q.sig["p_div"].sem, 1)
                yield at + 0.6
                dve.wait_ge(*q.sig["p_div"].at(g, 2 * t + 1))
                dve.reciprocal(sm, sm).then_inc(q.sig["p_div"].sem, 1)
                dve.wait_ge(*q.sig["p_div"].at(g, 2 * t + 2))
                dve.tensor_tensor(p, p, sm.unsqueeze(2).to_broadcast([P, NH, N]), ALU.mult).then_inc(q.sig["p_norm"].sem, 1)

            yield from softmax_front(0, 9.8)
            yield from softmax_front(1, 11.8)
            yield from softmax_back(0, 13.7)
            yield from softmax_back(1, 15.1)
            for k in range(KC):
                yield 20.0 + 0.4 * k
                dve.wait_ge(*q.sig["o_hi"].at(g, k + 1))
                dve.scalar_tensor_tensor(out=q.xt_l[:, k, :], in0=q.bank[:, 2 + k, 0:R], scalar=0.0, in1=f32(q.xt_h[:, k, :]),
                                         op0=ALU.max, op1=ALU.subtract).then_inc(q.sig["o_lo"].sem, 1)
            yield 22.2
            dve.wait_ge(*q.sig["y_ps"].at(g, 1))
            dve.tensor_tensor(q.u_sb[:, :, :], q.xin[:, :, :], q.bank[:, 0, :].rearrange("p (t d) -> p t d", t=TILES), ALU.add).then_inc(q.sig["u"].sem, 1)
            yield 22.9
            dve.wait_ge(q.sig["out"].sem, 16 * g + 1)
            yield from dve_norm(dve, q, g, 0, 22.9, q.xrow)

        def l0_gpsimd(pool, q, g):
            yield 0.0
            pool.wait_ge(*q.sig["load"].at(g, 32))
            pool.sem_inc(gate["pool"], 1)
            pool.tensor_copy(q.adjf_sb[:, :, :], q.adji[:, :, :]).then_inc(q.sig["adjf"].sem, 1)
            pool.wait_ge(*q.sig["adjf"].at(g, 1))
            pool.sem_inc(gate["pool"], 1)
            pool.tensor_scalar(q.negc[:, :, :], q.adjf_sb[:, :, :], 0.0, MASKED, ALU.is_equal, ALU.mult).then_inc(q.sig["mask"].sem, 1)
            pool.tensor_scalar(q.negm[:, :, 0:N], q.adjf_sb[:, :, :], 0.0, MASKED, ALU.is_equal, ALU.mult).then_inc(q.sig["mask"].sem, 1)
            pool.wait_ge(*q.sig["mask"].at(g, 2))
            pool.sem_inc(gate["pool"], 1)
            pool_spread(pool, q, q.negm)
            yield from pool_norm(pool, q, g, 0, 22.9)

        def pool_spread(pool, q, neg):
            for b in (1, 0):
                pool.tensor_scalar(neg[:, :, b * N:(b + 1) * N], neg[:, :, 0:N], other[:, b:b + 1], None, ALU.add).then_inc(q.sig["mask"].sem, 1)

        def l1_tensor(pe, q, g):
            yield 0.0
            pe.wait_ge(*q.sig["z"].at(g, TILES))
            pe_xt(pe, q, g, 1, q.xrow)
            yield 2.1
            pe_wait_xt(pe, q, g, 1)
            pe_rows(pe, q, 2, W1H).then_inc(q.sig["wh_ps"].sem, 1)
            yield 3.4
            pe_rep(pe, q, 0)
            yield 4.1
            pe.wait_ge(*q.sig["mask"].at(g, 7))
            for t in range(TILES):
                ins = pe.transpose(q.bank[:, 3, t * P:(t + 1) * P], q.neg1[:, t, :], ident[:, :])
            ins.then_inc(q.sig["negt_ps"].sem, 1)
            yield 8.3
            pe.wait_ge(*q.sig["e_norm"].at(g, 2))
            pe_agg(pe, q, (0, 0), q.scores[:, :, :].rearrange("p t j -> p (t j)"), q.val)

        def l1_scalar(act, q, g):
            yield from act_xt(act, q, g, 1)
            yield 3.5
            act.wait_ge(*q.sig["wh_ps"].at(g, 1))
            act.activation(q.val[:, :, :].rearrange("p t d -> p (t d)"), q.bank[:, 2, :], ACT.Copy).then_inc(q.sig["wh_sb"].sem, 1)
            yield 4.9
            act.wait_ge(*q.sig["lin_ps"].at(g, 1))
            for t in range(TILES):
                act.wait_ge(*q.sig["sc_dot"].at(g, t + 1))
                act.activation(q.scores[:, t, :], q.bank[:, 1, t * P:(t + 1) * P], ACT.Identity, bias=q.sc[:, t:t + 1]).then_inc(q.sig["lin"].sem, 1)
            yield 6.8
            act_exp(act, q, g, 0)
            yield 9.2
            act.wait_ge(*q.sig["agg_ps"].at(g, 2))
            act.activation(q.u_sb[:, :, :].rearrange("p t d -> p (t d)"), q.bank[:, 0, :], ACT.Copy).then_inc(q.sig["h1_sb"].sem, 1)

        def l1_vector(dve, q, g):
            yield from dve_xt(dve, q, g, 1)
            yield 4.1
            dve.wait_ge(*q.sig["wh_sb"].at(g, 1))
            for t in range(TILES):
                dve.tensor_tensor_reduce(out=q.val_sw[:, t, :], in0=q.val[:, t, :], in1=row[:, R_A2, :], scale=1.0, scalar=0.0,
                                         op0=ALU.mult, op1=ALU.add, accum_out=q.sc[:, t:t + 1]).then_inc(q.sig["sc_dot"].sem, 1)
            yield from dve_leaky(dve, q, g, 0, 5.6)
            dve.wait_ge(*q.sig["negt_ps"].at(g, 1))
            yield from dve_mask_max(dve, q, g, 0, 6.3, q.scores[:, :, :], q.bank[:, 3, 0:TILES * P].rearrange("p (t j) -> p t j", t=TILES))
            yield 7.7
            dve_inv(dve, q, g, 0)
            dve.wait_ge(*q.sig["e_inv"].at(g, 1))
            for t in range(TILES):
                dve.tensor_scalar(q.scores[:, t, :], q.scores[:, t, :], q.sm[:, t:t + 1], None, ALU.mult).then_inc(q.sig["e_norm"].sem, 1)
            yield 9.8
            dve.wait_ge(*q.sig["h1_sb"].at(g, 1))
            dve.scalar_tensor_tensor(out=q.u_sb[:, :, :], in0=q.u_sb[:, :, :], scalar=0.2, in1=q.u_sb[:, :, :],
                                     op0=ALU.mult, op1=ALU.max).then_inc(q.sig["leaky"].sem, 1)
            yield 10.4
            dve.wait_ge(*q.sig["leaky"].at(g, 1))
            dve.tensor_tensor(q.u_sb[:, :, :], q.u_sb[:, :, :], q.xrow[:, :, :], ALU.add).then_inc(q.sig["u"].sem, 1)
            yield 11.1
            yield from dve_norm(dve, q, g, 1, 11.1, q.xrow)

        def l1_gpsimd(pool, q, g):
            yield 0.1
            pool.wait_ge(*q.sig["z"].at(g, TILES))
            pool.sem_inc(gate["pool"], 1)
            pool.tensor_scalar(q.neg1[:, :, 0:N], q.adjf_sb[:, :, :], 0.0, MASKED_L1, ALU.is_le, ALU.mult).then_inc(q.sig["mask"].sem, 1)
            pool.wait_ge(*q.sig["mask"].at(g, 5))
            pool.sem_inc(gate["pool"], 1)
            pool_spread(pool, q, q.neg1)
            yield from pool_norm(pool, q, g, 1, 11.1)

        def l2_tensor(pe, q, g):
            yield 0.0
            pe.wait_ge(*q.sig["z"].at(g, 2 * TILES))
            pe_xt(pe, q, g, 2, q.xrow)
            yield 2.1
            pe_wait_xt(pe, q, g, 2)
            pe_cols(pe, q, 1, W2T).then_inc(q.sig["h_ps"].sem, 1)
            yield 3.4
            pe_cols(pe, q, 2, W2M).then_inc(q.sig["h_ps"].sem, 1)
            yield 4.7
            pe_rows(pe, q, 3, W2T).then_inc(q.sig["h_ps"].sem, 1)
            yield 6.0
            pe.wait_ge(*q.sig["h_sb"].at(g, 2))
            pe.wait_ge(*q.sig["ha_sb"].at(g, 2))
            for t in range(TILES):
                for k in range(KC):
                    ins = pe.matmul(q.bank[:, 0, t * P:(t + 1) * P], q.work[:, KC + k, t * P:(t + 1) * P], q.work[:, k, t * P:(t + 1) * P],
                                    start=(k == 0), stop=(k == KC - 1))
            ins.then_inc(q.sig["sc_ps"].sem, 1)
            yield 8.7
            pe_pt(pe, q, g, 1, 1)
            yield 9.6
            pe.wait_ge(*q.sig["pt_sb"].at(g, 1))
            pe.wait_ge(*q.sig["hrow_sb"].at(g, 1))
            pe_agg(pe, q, (2, 2), q.pt, q.val)

        def l2_scalar(act, q, g):
            yield from act_xt(act, q, g, 2)
            yield 3.5
            act.wait_ge(*q.sig["h_ps"].at(g, 1))
            for o in range(KC):
                act.activation(q.work[:, o, :], q.bank[:, 1, o * R:(o + 1) * R], ACT.Identity, bias=col[:, C_LB + o:C_LB + o + 1]).then_inc(q.sig["h_sb"].sem, 1)
            yield 7.9
            act_exp(act, q, g, 1)
            yield 9.2
            act_pt(act, q, g, 1, 1)
            yield 11.7
            act.wait_ge(*q.sig["elu_m"].at(g, 1))
            m = q.work[:, 0:TILES, :]
            act.activation(m, m, ACT.Exp).then_inc(q.sig["elu_e"].sem, 1)

        def l2_vector(dve, q, g):
            yield from dve_xt(dve, q, g, 2)
            yield 4.8
            dve.wait_ge(*q.sig["h_ps"].at(g, 2))
            for o in range(KC):
                dve.tensor_scalar(q.work[:, KC + o, :], q.bank[:, 2, o * R:(o + 1) * R], mcol[:, o:o + 1], None, ALU.add).then_inc(q.sig["ha_sb"].sem, 1)
            yield 6.1
            dve.wait_ge(*q.sig["h_ps"].at(g, 3))
            dve.tensor_tensor(q.val[:, :, :], q.bank[:, 3, :].rearrange("p (t d) -> p t d", t=TILES),
                              row[:, R_LB:R_LB + 1, :].to_broadcast([P, TILES, D]), ALU.add).then_inc(q.sig["hrow_sb"].sem, 1)
            yield 7.0
            dve.wait_ge(*q.sig["sc_ps"].at(g, 1))
            dve.wait_ge(*q.sig["mask"].at(g, 4))
            yield from dve_mask_max(dve, q, g, 1, 7.4, q.bank[:, 0, 0:TILES * P].rearrange("p (t j) -> p t j", t=TILES), q.negm[:, :, :])
            yield 8.8
            dve_inv(dve, q, g, 1)
            yield 10.5
            dve.wait_ge(*q.sig["agg_ps"].at(g, 4))
            dve.wait_ge(*q.sig["e_inv"].at(g, 2))
            for t in range(TILES):
                dve.tensor_scalar(q.u_sb[:, t, :], q.bank[:, 2, t * D:(t + 1) * D], q.sm[:, t:t + 1], None, ALU.mult).then_inc(q.sig["elu"].sem, 1)
            yield 11.2
            dve.wait_ge(*q.sig["elu"].at(g, 2))
            dve.tensor_scalar(q.work[:, 0:TILES, :], q.u_sb[:, :, :], 0.0, None, ALU.min).then_inc(q.sig["elu_m"].sem, 1)
            yield 12.3
            dve.wait_ge(*q.sig["elu_e"].at(g, 1))
            dve.scalar_tensor_tensor(out=q.u_sb[:, :, :], in0=q.u_sb[:, :, :], scalar=0.0, in1=q.work[:, 0:TILES, :],
                                     op0=ALU.max, op1=ALU.add).then_inc(q.sig["elu"].sem, 1)
            yield 12.9
            dve.wait_ge(*q.sig["elu"].at(g, 3))
            dve.scalar_tensor_tensor(out=q.u_sb[:, :, :], in0=q.u_sb[:, :, :], scalar=-1.0, in1=q.xrow[:, :, :],
                                     op0=ALU.add, op1=ALU.add).then_inc(q.sig["u"].sem, 1)
            yield 13.5
            yield from dve_norm(dve, q, g, 2, 13.5, q.xkeep)

        def l2_gpsimd(pool, q, g):
            yield 8.0
            pool.wait_ge(*q.sig["e_add"].at(g, 2))
            pool.tensor_tensor(q.adjf_sb[:, :, :], q.adjf_sb[:, :, :], eye[:, :].unsqueeze(1).to_broadcast([P, TILES, N]), ALU.add).then_inc(q.sig["mask"].sem, 1)
            pool.wait_ge(*q.sig["mask"].at(g, 8))
            pool.sem_inc(gate["pool"], 1)
            pool.tensor_scalar(q.negm[:, :, 0:N], q.adjf_sb[:, :, :], 0.0, MASKED, ALU.is_le, ALU.mult).then_inc(q.sig["mask"].sem, 1)
            pool.wait_ge(*q.sig["mask"].at(g, 9))
            pool.sem_inc(gate["pool"], 1)
            pool_spread(pool, q, q.negm)
            yield from pool_norm(pool, q, g, 2, 13.5)

        def at_tensor(pe, q, g, l):
            yield 0.0
            pe.wait_ge(*q.sig["z"].at(g, TILES * (3 + 2 * l)))
            pe_xt(pe, q, g, 3 + 2 * l, q.u_sb if l else q.xkeep)
            yield 2.1
            pe_wait_xt(pe, q, g, 3 + 2 * l)
            pe_rep(pe, q, 1 + l)
            yield 5.5
            pe_pt(pe, q, g, 2 + l, 2)
            yield 6.4
            pe.wait_ge(*q.sig["pt_sb"].at(g, 2 + l))
            if l:
                pe.wait_ge(*q.sig["aff"].at(g, 2 * l))
            pe_agg(pe, q, (3, 0), q.pt, q.xrow if l else q.xkeep)

        def at_scalar(act, q, g, l):
            yield from act_xt(act, q, g, 3 + 2 * l)
            yield 2.9
            act.wait_ge(*q.sig["lin_ps"].at(g, 2 + l))
            act.wait_ge(*q.sig["sc_ready"].at(g, 1 + l))
            for t in range(TILES):
                act.activation(q.scores[:, t, :], q.bank[:, 1, t * P:(t + 1) * P], ACT.Identity, bias=q.sc[:, t:t + 1]).then_inc(q.sig["lin"].sem, 1)
            yield 4.8
            act_exp(act, q, g, 2 + l)
            yield 6.0
            act_pt(act, q, g, 2 + l, 2)

        def at_vector(dve, q, g, l):
            src = q.u_sb if l else q.xkeep
            yield 0.0
            dve.wait_ge(*q.sig["z"].at(g, TILES * (3 + 2 * l)))
            for t in range(TILES):
                dve.tensor_tensor_reduce(out=q.val[:, t, :], in0=src[:, t, :], in1=row[:, R_WI + l, :], scale=1.0, scalar=0.0,
                                         op0=ALU.mult, op1=ALU.add, accum_out=q.sc[:, t:t + 1]).then_inc(q.sig["sc_dot"].sem, 1)
            yield from dve_xt(dve, q, g, 3 + 2 * l)
            yield 1.9
            dve.wait_ge(*q.sig["sc_dot"].at(g, TILES * (2 + l)))
            dve.tensor_scalar(q.sc[:, :], q.sc[:, :], abias[:, l:l + 1], None, ALU.add).then_inc(q.sig["sc_ready"].sem, 1)
            yield from dve_leaky(dve, q, g, 1 + l, 3.5)
            if l == 0:
                dve.wait_ge(*q.sig["mask"].at(g, 11))
            yield from dve_mask_max(dve, q, g, 2 + l, 4.3, q.scores[:, :, :], q.negm[:, :, :])
            yield 5.6
            dve_inv(dve, q, g, 2 + l)
            rows_ = q.xrow if l else q.xkeep
            for t in range(TILES):
                yield 7.1 + 0.4 * t
                dve.wait_ge(*q.sig["agg_ps"].at(g, TILES * (2 + l) + t + 1))
                dve.wait_ge(*q.sig["e_inv"].at(g, 3 + l))
                dve.scalar_tensor_tensor(out=q.u_sb[:, t, :], in0=q.bank[:, 3 - 3 * t, t * D:(t + 1) * D], scalar=q.sm[:, t:t + 1], in1=rows_[:, t, :],
                                         op0=ALU.mult, op1=ALU.add).then_inc(q.sig["u" if t else "u_b"].sem, 1)
            yield 8.1
            dve.wait_ge(*q.sig["u_b"].at(g, 1 + l))
            yield from dve_norm(dve, q, g, 3 + 2 * l, 8.1, q.u_sb)

        def at_gpsimd(pool, q, g, l):
            if l:
                yield 0.0
                pool.wait_ge(*q.sig["z"].at(g, TILES * (3 + 2 * l)))
                pool_affine(pool, q, g, l - 1, q.xrow, R_G2, R_B2, "aff")
            yield from pool_norm(pool, q, g, 3 + 2 * l, 8.1)

        LAGC = 3

        F_BANKS = (1, 2, 0)

        def ff_due(f):
            return 2.1 + 0.65 * min(f, LAGC) + 1.3 * max(f - LAGC, 0)

        def ff_tensor(pe, q, g, l):
            yield 0.0
            pe.wait_ge(*q.sig["z"].at(g, TILES * (4 + 2 * l)))
            pe_xt(pe, q, g, 4 + 2 * l, q.u_sb)
            for f in range(FC + LAGC):
                if f < FC:
                    yield ff_due(f)
                    if f == 0:
                        pe_wait_xt(pe, q, g, 4 + 2 * l)
                    if f >= 3:
                        pe.wait_ge(*q.sig["ff_gelu"].at(g, l * FC + f - 2))
                    for k in range(KC):
                        ins = split3(pe, q.bank[:, F_BANKS[f % 3], 0:R], w1_h[:, l, k, f * P:(f + 1) * P], w1_l[:, l, k, f * P:(f + 1) * P],
                                     q.xt_h[:, k, :], q.xt_l[:, k, :], k == 0, k == KC - 1)
                    ins.then_inc(q.sig["f_ps"].sem, 1)
                if f >= LAGC:
                    c = f - LAGC
                    yield ff_due(FC) + 0.65 * (f - FC) if f >= FC else ff_due(f) + 0.65
                    pe.wait_ge(*q.sig["ff_lo"].at(g, l * FC + c + 1))
                    for t in range(TILES):
                        ins = split3(pe, q.bank[:, 3, t * D:(t + 1) * D], q.g_hi[:, c % 2, t * P:(t + 1) * P], q.g_lo[:, c % 2, t * P:(t + 1) * P],
                                     w2_h[:, l, c, :], w2_l[:, l, c, :], c == 0, c == FC - 1, start=(t == 0))
                    ins.then_inc(q.sig["ff_used"].sem, 1)

        def ff_scalar(act, q, g, l):
            yield from act_xt(act, q, g, 4 + 2 * l)
            for f in range(FC):
                yield ff_due(f) + 0.7
                act.wait_ge(*q.sig["f_ps"].at(g, l * FC + f + 1))
                if f >= 4:
                    act.wait_ge(*q.sig["ff_lo"].at(g, l * FC + f - 3))
                act.activation(q.work[:, f % 4, :], q.bank[:, F_BANKS[f % 3], 0:R], ACT.Gelu, bias=ffb[:, l * FC + f:l * FC + f + 1]).then_inc(q.sig["ff_gelu"].sem, 1)

        def ff_vector(dve, q, g, l):
            yield from dve_xt(dve, q, g, 4 + 2 * l)
            for f in range(FC):
                yield max(ff_due(f) + 1.2, ff_due(f - 2 + LAGC) + 0.65 if f >= 2 and f + 1 < FC else ff_due(FC) if f >= 2 else 0)
                if f >= 2:
                    dve.wait_ge(*q.sig["ff_used"].at(g, l * FC + f - 1))
                dve.wait_ge(*q.sig["ff_gelu"].at(g, l * FC + f + 1))
                dve.tensor_copy(q.g_hi[:, f % 2, :], q.work[:, f % 4, :]).then_inc(q.sig["ff_hi"].sem, 1)
                dve.wait_ge(*q.sig["ff_hi"].at(g, l * FC + f + 1))
                dve.tensor_tensor(q.g_lo[:, f % 2, :], q.work[:, f % 4, :], f32(q.g_hi[:, f % 2, :]), ALU.subtract).then_inc(q.sig["ff_lo"].sem, 1)
            at = ff_due(FC) + 0.65 * LAGC
            yield at
            dve.wait_ge(*q.sig["ff_used"].at(g, (l + 1) * FC))
            dve.wait_ge(*q.sig["hb"].at(g, 2 * l + 2))
            dve.tensor_tensor(q.u_sb[:, :, :], q.val_sw[:, :, :], q.bank[:, 3, :].rearrange("p (t d) -> p t d", t=TILES), ALU.add).then_inc(q.sig["u"].sem, 1)
            yield at + 0.6
            yield from dve_norm(dve, q, g, 4 + 2 * l, at + 0.6, q.u_sb)
            if l == L - 1:
                yield at + 5.5
                dve.wait_ge(*q.sig["aff"].at(g, 2 * L))
                dve.tensor_tensor(q.u_sb[:, :, :], q.xrow[:, :, :], q.xkeep[:, :, :], ALU.add).then_inc(q.sig["u"].sem, 1)
                yield at + 6.1
                yield from dve_norm(dve, q, g, 9, at + 6.1, q.xrow)

        def ff_gpsimd(pool, q, g, l):
            yield 0.0
            pool.wait_ge(*q.sig["z"].at(g, TILES * (4 + 2 * l)))
            pool_affine(pool, q, g, l, q.val_sw, R_G1, R_B1, "hb")
            at = ff_due(FC) + 0.65 * LAGC
            yield from pool_norm(pool, q, g, 4 + 2 * l, at + 0.6)
            if l == L - 1:
                yield at + 2.8
                pool.wait_ge(*q.sig["z"].at(g, TILES * (5 + 2 * l)))
                pool_affine(pool, q, g, l, q.xrow, R_G2, R_B2, "aff")
                yield from pool_norm(pool, q, g, 9, at + 6.1)

        def sync_out(sp, q, g):
            yield ff_due(FC) + 0.65 * LAGC + 8.7
            sp.wait_ge(*q.sig["z"].at(g, 10 * TILES))
            sp.sem_inc(gate["sp"], 1)
            sp.dma_start(out_v[2 * g + q.s], q.xrow[:, :, :]).then_inc(q.sig["out"].sem, 16)

        def sync_load(sp, q, g):
            sp.dma_start(q.xin[:, :, :], x_v[2 * g + q.s]).then_inc(q.sig["load"].sem, 16)
            sp.dma_start(q.adji[:, :, :], adj_v[2 * g + q.s]).then_inc(q.sig["load"].sem, 16)

        STEPS = {
            "tensor": (l0_tensor, l1_tensor, l2_tensor, at_tensor, ff_tensor),
            "scalar": (l0_scalar, l1_scalar, l2_scalar, at_scalar, ff_scalar),
            "vector": (l0_vector, l1_vector, l2_vector, at_vector, ff_vector),
            "gpsimd": (l0_gpsimd, l1_gpsimd, l2_gpsimd, at_gpsimd, ff_gpsimd),
        }
        LENGTH = (25.6, 13.8, 16.2) + (10.8, 15.9) * (L - 1) + (10.8, 22.0)

        def phase(eng, kind, ph, q, g, more):
            if kind == "sync":
                if ph == 4 and more:
                    yield 0.0
                    eng.wait_ge(*q.sig["u"].at(g, 1))
                    eng.sem_inc(gate["sp"], 1)
                    eng.wait_ge(*q.sig["adjf"].at(g, 1))
                    eng.sem_inc(gate["sp"], 1)
                    sync_load(eng, q, g + 1)
                if ph == PHASES - 1:
                    yield from sync_out(eng, q, g)
            elif ph < 3:
                yield from STEPS[kind][ph](eng, q, g)
            elif ph % 2:
                yield from STEPS[kind][3](eng, q, g, (ph - 3) // 2)
            else:
                yield from STEPS[kind][4](eng, q, g, (ph - 4) // 2)

        def run_phases(eng, kind, q, todo, start=0.0):
            for ph, g, more in todo:
                if not isinstance(g, int) and kind != "sync":
                    own = eng.alloc_register(f"{kind}_{q.s}_{ph}")
                    eng.reg_mov(own, g)
                    g = eng.snap(own, donate=True, min_val=0, max_val=groups - 1)
                for due in phase(eng, kind, ph, q, g, more):
                    yield start + due
                start += LENGTH[ph]

        A, B = streams
        LEAD = 4

        def whole(eng, kind):
            merged(iter(()), run_phases(eng, kind, B, [(ph, 0, True) for ph in range(LEAD)]))

            def period(i, last):
                late = [(ph, i, not last) for ph in range(LEAD, PHASES)]
                early = [] if last else [(ph, i + 1, True) for ph in range(LEAD)]
                merged(run_phases(eng, kind, A, [(ph, i, not last) for ph in range(PHASES)]),
                       run_phases(eng, kind, B, late + early))

            with eng.Fori(0, groups - 1) as i:
                period(i, False)
            period(groups - 1, True)

        @block.sync
        def _(sp):
            prep_sync(sp)
            for q in (B, A):
                sync_load(sp, q, 0)
                sp.sem_inc(q.sig["out"].sem, 1)
            whole(sp, "sync")
            for q in (A, B):
                sp.wait_ge(q.sig["out"].sem, 16 * groups + 1)

        @block.gpsimd
        def _(pool):
            prep_gpsimd(pool)
            pool.wait_ge(consts, 1)
            whole(pool, "gpsimd")

        @block.scalar
        def _(act):
            prep_scalar(act)
            act.wait_ge(consts, 1)
            whole(act, "scalar")

        @block.vector
        def _(dve):
            prep_vector(dve)
            dve.wait_ge(consts, 1)
            whole(dve, "vector")

        @block.tensor
        def _(pe):
            prep_tensor(pe)
            pe.wait_ge(consts, 1)
            pe.wait_ge(ident_ready, 3)
            whole(pe, "tensor")


_SMALL = (("L0_gnn_Wq", "L0_gnn_Wk"), ("L0_gnn_Wv", "L0_gnn_Wo"), ("L1_gnn_W", "L2_gnn_W^T"), ("L2_gnn_W", "L2_gnn_attn"))


def kernel(**inputs):
    import numpy as np
    import concourse.bacc as bacc
    from concourse.bass_utils import run_bass_kernel_spmd as run

    a = {k: np.asarray(v) for k, v in inputs.items()}
    x = a["x"]
    B, n, d = x.shape

    def by_partition(v):
        return v.reshape(-1, P).T

    get = lambda name: a[name[:-2]].T if name.endswith("^T") else a[name]
    w = a["L3_gnn_attn_w"]
    cols = np.concatenate([
        by_partition(a["L3_gnn_b1"]), by_partition(a["L3_gnn_beta1"]), by_partition(a["L3_gnn_g1"]),
        by_partition(w[:, d:]), by_partition(a["L2_gnn_b"]), np.broadcast_to(a["L3_gnn_attn_b"], (P, L)),
        by_partition(a["L3_gnn_g2"])], axis=1)
    rows = np.concatenate([
        w[:, :d], a["L3_gnn_g1"], a["L3_gnn_beta1"], a["L3_gnn_g2"], a["L3_gnn_beta2"],
        a["L1_gnn_a"][d:].reshape(1, d), a["L2_gnn_b"].reshape(1, d)], axis=0)
    prep_rows = np.concatenate([a["L1_gnn_a"][:d].reshape(1, d), a["L3_gnn_b2"], w[1:, d:]], axis=0)
    arrays = {
        "x_in": x.reshape(B * n, d),
        "adj_in": a["adj"].reshape(B * n, n),
        "w_small": np.stack([np.concatenate([get(u), get(v)], axis=0) for u, v in _SMALL]),
        "w1": a["L3_gnn_W1"],
        "w2": a["L3_gnn_W2"],
        "cols": cols,
        "rows": rows,
        "prep_rows": prep_rows,
    }
    arrays = {k: np.ascontiguousarray(v) for k, v in arrays.items()}
    nc = bacc.Bacc("TRN2", target_bir_lowering=False, num_devices=1)
    args = [nc.dram_tensor(k, v.shape, mybir.dt.from_np(v.dtype), kind="ExternalInput").ap() for k, v in arrays.items()]
    out = nc.dram_tensor("out", (B * n, d), F32, kind="ExternalOutput").ap()
    gnn_kernel(nc, *args, out)
    r = run(nc, [arrays], core_ids=[0])
    return r.results[0]["out"].reshape(B, n, d)
```

```python
from contextlib import ExitStack

import concourse.bass as bass
from concourse import mybir

F32 = mybir.dt.float32
F32R = mybir.dt.float32r
I32 = mybir.dt.int32
ALU = mybir.AluOpType
ACT = mybir.ActivationFunctionType
AX_X = mybir.AxisListType.X

P = 128
D = 256
KC = D // P
N = 64
TILES = 2
R = TILES * P
NH = 8
DK = D // NH
RG = 4
HC = NH // RG
L = 3
FF = 4 * D
FC = FF // P
EPS = 1e-5
MASKED = -1e30
OTHER = -3e38
MASKED_L1 = -9e15
WQ, WK, WV, WO, W1H, W2T, W2M = range(7)
R_WI, R_WJ, R_G1, R_B1, R_G2, R_B2, R_A2, R_LB = 0, L, 2 * L, 3 * L, 4 * L, 5 * L, 6 * L, 6 * L + 1
ROWS = 6 * L + 2
PHASES = 9
TAIL = PHASES


class Stream:
    pass


class Signal:

    def __init__(self, sem, per):
        self.sem, self.per = sem, per

    def at(self, g, k):
        return self.sem, g * self.per + k


def merged(*tracks):
    due = [next(t, None) for t in tracks]
    while any(d is not None for d in due):
        n = min((d, n) for n, d in enumerate(due) if d is not None)[1]
        due[n] = next(tracks[n], None)


def gnn_kernel(nc, x, adj, w_small, w1, w2, cols, rows, prep_rows, out):
    groups = x.shape[0] // (2 * R)
    x_v = x.rearrange("(n t p) d -> n p t d", t=TILES, p=P)
    out_v = out.rearrange("(n t p) d -> n p t d", t=TILES, p=P)
    adj_v = adj.rearrange("(n t p) j -> n p t j", t=TILES, p=P)
    C_FB, C_BETA1, C_G1 = 0, L * FC, L * (FC + KC)
    C_LB = C_G1 + L * KC
    C_AB = C_LB + KC
    NCOLS = C_AB + L

    with ExitStack() as ctx:
        def sb(name, shape, dt=F32):
            return ctx.enter_context(nc.sbuf_tensor(name, shape, dt))

        def sem(name):
            return ctx.enter_context(nc.semaphore(name))

        ws_h = sb("ws_h", [P, 7, KC, D], F32R)
        ws_l = sb("ws_l", [P, 7, KC, D], F32R)
        w1_h = sb("w1_h", [P, L, KC, FF], F32R)
        w1_l = sb("w1_l", [P, L, KC, FF], F32R)
        w2_h = sb("w2_h", [P, L, FC, D], F32R)
        w2_l = sb("w2_l", [P, L, FC, D], F32R)
        rep_h = sb("rep_h", [P, KC, P], F32R)
        rep_l = sb("rep_l", [P, KC, P], F32R)
        col = sb("col", [P, NCOLS])
        row = sb("row", [P, ROWS, D])
        ident = sb("ident", [P, P])
        eye = sb("eye", [P, N])
        ffb = sb("ffb", [P, L * FC])
        mcol = sb("mcol", [P, KC])
        wa1 = sb("wa1", [P, KC])
        other = sb("other", [P, 2])
        abias = sb("abias", [P, L])
        mhalf = sb("mhalf", [P, TILES])

        w_in = [sem(f"w_in{i}") for i in range(2)]
        c_in = sem("c_in")
        ones_ready = sem("ones_ready")
        ident_ready = sem("ident_ready")
        w_hi = sem("w_hi")
        w_lo = sem("w_lo")
        w_used = sem("w_used")
        prep_dve = sem("prep_dve")
        prep_act = sem("prep_act")
        prep_pe = sem("prep_pe")
        consts = sem("consts")
        gate = {name: sem(f"gate_{name}") for name in ("pe", "dve", "pool", "sp")}
        streams = []
        for s in range(2):
            q = Stream()
            q.sig = {name: Signal(sem(f"{name}_{s}"), per) for name, per in dict(
                load=32, out=16, adjf=1, mask=11,
                xt_ps=12, xt_hi=12, xt_lo=12,
                qkv_ps=3, qk_sb=2, v_sb=1, vsw_sb=2,
                s_ps=1, p_add=2, p_max=2, p_sub=2, p_exp=2, p_div=4, p_norm=2,
                pt0_ps=2, pt0_sb=2, pv0_ps=2, o_hi=2, o_lo=2, y_ps=1,
                negt_ps=1, lin_ps=4, wh_ps=1, wh_sb=1, sc_dot=14, sc_ready=3, lin=8,
                h_ps=3, h_sb=2, ha_sb=2, hrow_sb=1, sc_ps=1,
                e_add=2, e_max=5, e_exp=10, e_inv=5, e_norm=2,
                pt_ps=4, pt_sb=4, agg_ps=10, leaky=1, h1_sb=1, leak=4, elu=3, elu_m=1, elu_e=1,
                u=10, st=20, mv=20, ve=10, rstd=10, z=20,
                hb=6, f_ps=24, ff_gelu=24, ff_hi=24, ff_lo=24, ff_used=24, u_b=3, aff=6,
            ).items()}
            q.s = s
            q.xin = sb(f"xin{s}", [P, TILES, D])
            q.xrow = sb(f"xrow{s}", [P, TILES, D])
            q.u_sb = sb(f"u{s}", [P, TILES, D])
            q.xkeep = sb(f"xkeep{s}", [P, TILES, D])
            q.xt_h = sb(f"xt_h{s}", [P, KC, R], F32R)
            q.xt_l = sb(f"xt_l{s}", [P, KC, R], F32R)
            q.val = sb(f"val{s}", [P, TILES, D])
            q.val_sw = sb(f"val_sw{s}", [P, TILES, D])
            q.work = sb(f"work{s}", [P, 4, R])
            q.pt = sb(f"pt{s}", [P, 4 * P])
            q.adji = sb(f"adji{s}", [P, TILES, N], I32)
            q.adjf_sb = sb(f"adjf{s}", [P, TILES, N])
            q.negc = sb(f"negc{s}", [P, TILES, N])
            q.neg1 = q.u_sb[:, :, 0:P]
            q.g_hi = sb(f"g_hi{s}", [P, 2, R], F32R)
            q.g_lo = sb(f"g_lo{s}", [P, 2, R], F32R)
            q.negm = sb(f"negm{s}", [P, TILES, P])
            q.mx = sb(f"mx{s}", [P, NH * TILES])
            q.sm = sb(f"sm{s}", [P, NH * TILES])
            q.stat = sb(f"stat{s}", [P, TILES, 6])
            q.mv_sb = sb(f"mv{s}", [P, TILES, 2])
            q.ve_sb = sb(f"ve{s}", [P, TILES])
            q.rstd_sb = sb(f"rstd{s}", [P, TILES])
            q.sc = sb(f"sc{s}", [P, TILES])
            q.sj = sb(f"sj{s}", [P, TILES])
            q.bank = ctx.enter_context(nc.psum_tensor(f"bank{s}", [P, 4, 512], F32))
            q.scores = q.pt[:, 2 * P:].rearrange("p (t j) -> p t j", t=TILES)
            streams.append(q)

        def f32(ap):
            return ap.bitcast(F32)

        def split3(pe, out_ap, lh, ll, rh, rl, first, last, start=True):
            pe.matmul(out_ap, lh, rh, start=first and start, stop=False, skip_group_check=True)
            pe.matmul(out_ap, lh, rl, start=False, stop=False, skip_group_check=True)
            return pe.matmul(out_ap, ll, rh, start=False, stop=last, skip_group_check=True)

        stage = [streams[u].work[:].rearrange("p a b -> p (a b)") for u in range(2)]
        units = [("small", i) for i in range(3)] + [("mix", 0)] + [("w1", l, k) for l in range(L) for k in range(KC)] \
            + [("w2", l, h) for l in range(L) for h in range(2)]

        block = ctx.enter_context(nc.Block())

        def unit_src(u):
            if u[0] in ("small", "mix"):
                i = u[1] if u[0] == "small" else 3
                return w_small[i].rearrange("(m k p) n -> p m k n", m=2, p=P), "p (m k n) -> p m k n", dict(m=2, k=KC)
            if u[0] == "w1":
                return w1[u[1], u[2] * P:(u[2] + 1) * P, :], None, None
            return w2[u[1], u[2] * 512:(u[2] + 1) * 512, :].rearrange("(f p) d -> p f d", p=P), "p (f d) -> p f d", dict(f=4)

        def unit_dst(u, part):
            ws, wa, wb = (ws_h, w1_h, w2_h) if part == "hi" else (ws_l, w1_l, w2_l)
            if u[0] == "small":
                return ws[:, 2 * u[1]:2 * u[1] + 2, :, :].rearrange("p m k n -> p (m k n)")
            if u[0] == "w1":
                return wa[:, u[1], u[2], :]
            return wb[:, u[1], 4 * u[2]:4 * u[2] + 4, :].rearrange("p f d -> p (f d)")

        def prep_sync(sp):
            sp.dma_start(col[:, :], cols).then_inc(c_in, 16)
            sp.dma_start(row[:, :, :], rows.partition_broadcast(P)).then_inc(c_in, 16)
            sp.dma_start(streams[0].xrow[:, 0, :], prep_rows[0].partition_broadcast(P)).then_inc(c_in, 16)
            sp.dma_start(streams[0].val[:, :, :], prep_rows[1:3].partition_broadcast(P)).then_inc(c_in, 16)
            sp.dma_start(streams[0].val_sw[:, 0, :], prep_rows[3].partition_broadcast(P)).then_inc(c_in, 16)
            for i, u in enumerate(units):
                src, pat, kw = unit_src(u)
                if i >= 2:
                    sp.wait_ge(w_lo, i - 1)
                    if 3 <= i - 2 < 4 + L * KC:
                        sp.wait_ge(w_used, i - 4)
                dst = stage[i % 2] if pat is None else stage[i % 2].rearrange(pat, **kw)
                sp.dma_start(dst, src).then_inc(w_in[i % 2], 16)

        def prep_scalar(act):
            act.wait_ge(c_in, 80)
            for i, u in enumerate(units):
                act.wait_ge(w_in[i % 2], 16 * (i // 2 + 1))
                if u[0] == "mix":
                    act.wait_ge(prep_pe, 1)
                    act.activation(ws_h[:, W2M, :, :].rearrange("p k n -> p (k n)"), streams[0].bank[:, 0, :], ACT.Copy).then_inc(w_hi, 1)
                elif u[0] == "w1":
                    c = C_G1 + u[1] * KC + u[2]
                    act.activation(unit_dst(u, "hi"), stage[i % 2], ACT.Copy, scale=col[:, c:c + 1]).then_inc(w_hi, 1)
                else:
                    act.activation(unit_dst(u, "hi"), stage[i % 2], ACT.Copy).then_inc(w_hi, 1)

        def prep_vector(dve):
            dve.wait_ge(c_in, 80)
            n = 0
            for b in range(2):
                dve.memset(other[b * N:(b + 1) * N, b:b + 1], 0.0).then_inc(prep_dve, 1)
                dve.memset(other[b * N:(b + 1) * N, 1 - b:2 - b], OTHER).then_inc(prep_dve, 1)
                n += 2
            dve.memset(mhalf[:, :], -0.5).then_inc(prep_dve, 1)
            ones = streams[0].pt[:, 0:P]
            dve.memset(ones, 1.0).then_inc(prep_dve, 1)
            n += 2
            dve.tensor_tensor(row[:, R_B1:R_B1 + 2, :], row[:, R_B1:R_B1 + 2, :], streams[0].val[:, :, :], ALU.add).then_inc(prep_dve, 1)
            dve.tensor_tensor(row[:, R_B1 + 2, :], row[:, R_B1 + 2, :], streams[0].val_sw[:, 0, :], ALU.add).then_inc(prep_dve, 1)
            n += 2
            dve.tensor_copy(abias[:, :], col[:, C_AB:C_AB + L]).then_inc(prep_dve, 1)
            n += 1
            for l in range(1, L):
                for part in (row[:, R_WI + l, :], row[:, R_WJ + l, :]):
                    dve.wait_ge(prep_dve, n)
                    dve.tensor_tensor_reduce(out=streams[0].u_sb[:, 0, :], in0=part, in1=row[:, R_B2 + l - 1, :], scale=1.0, scalar=abias[:, l:l + 1],
                                             op0=ALU.mult, op1=ALU.add, accum_out=abias[:, l:l + 1]).then_inc(prep_dve, 1)
                    n += 1
                dve.wait_ge(prep_dve, n)
                for r in (R_WI + l, R_WJ + l):
                    dve.tensor_tensor(row[:, r, :], row[:, r, :], row[:, R_G2 + l - 1, :], ALU.mult).then_inc(prep_dve, 1)
                    n += 1
            for i, u in enumerate(units):
                raw = stage[i % 2]
                dve.wait_ge(w_in[i % 2], 16 * (i // 2 + 1))
                dve.wait_ge(w_hi, i + 1)
                if u == ("small", 2):
                    for k in range(KC):
                        dve.wait_ge(prep_dve, n)
                        dve.tensor_tensor_reduce(out=streams[0].u_sb[:, 0, :], in0=raw[:, k * D:(k + 1) * D], in1=streams[0].xrow[:, 0, :],
                                                 scale=1.0, scalar=0.0, op0=ALU.mult, op1=ALU.add,
                                                 accum_out=wa1[:, k:k + 1]).then_inc(prep_dve, 1)
                        n += 1
                if u[0] == "mix":
                    dve.tensor_tensor(ws_l[:, W2M, :, :].rearrange("p k n -> p (k n)"), streams[0].bank[:, 0, :],
                                      f32(ws_h[:, W2M, :, :]).rearrange("p k n -> p (k n)"), ALU.subtract).then_inc(w_lo, 1)
                elif u[0] == "w1":
                    c = C_G1 + u[1] * KC + u[2]
                    dve.scalar_tensor_tensor(out=unit_dst(u, "lo"), in0=raw, scalar=col[:, c:c + 1], in1=f32(unit_dst(u, "hi")),
                                             op0=ALU.mult, op1=ALU.subtract).then_inc(w_lo, 1)
                else:
                    dve.tensor_tensor(unit_dst(u, "lo"), raw, f32(unit_dst(u, "hi")), ALU.subtract).then_inc(w_lo, 1)
            dve.wait_ge(prep_dve, n)
            for k in range(KC):
                dve.tensor_scalar(rep_h[:, k, :], ones, wa1[:, k:k + 1], None, ALU.mult).then_inc(prep_dve, 1)
                n += 1
                dve.wait_ge(prep_dve, n)
                dve.scalar_tensor_tensor(out=rep_l[:, k, :], in0=ones, scalar=wa1[:, k:k + 1], in1=f32(rep_h[:, k, :]),
                                         op0=ALU.mult, op1=ALU.subtract).then_inc(prep_dve, 1)
                n += 1
            dve.wait_ge(w_used, 1)
            dve.tensor_copy(mcol[:, :], streams[0].bank[:, 1, 0:KC]).then_inc(prep_dve, 1)
            dve.wait_ge(w_used, 1 + L * KC)
            dve.tensor_tensor(ffb[:, :], streams[1].bank[:, 0, 0:L * FC], col[:, C_FB:C_FB + L * FC], ALU.add).then_inc(prep_dve, 1)
            n += 2
            dve.wait_ge(prep_dve, n)
            dve.engine_nop().then_inc(consts, 1)

        def prep_tensor(pe):
            pe.wait_ge(c_in, 80)
            for i, u in enumerate(units):
                raw = stage[i % 2]
                pe.wait_ge(w_in[i % 2], 16 * (i // 2 + 1))
                if u[0] == "mix":
                    m = raw.rearrange("p (m k n) -> p m k n", m=2, k=KC)
                    for i2 in range(KC):
                        for o in range(KC):
                            ins = pe.matmul(streams[0].bank[:, 0, i2 * D:(i2 + 1) * D], m[:, 0, o, i2 * P:(i2 + 1) * P], m[:, 1, o, :],
                                            start=(o == 0), stop=(o == KC - 1))
                    ins.then_inc(prep_pe, 1)
                    for j in range(KC):
                        for o in range(KC):
                            ins = pe.matmul(streams[0].bank[:, 1, j:j + 1], m[:, 1, o, j * P:(j + 1) * P], col[:, C_LB + o:C_LB + o + 1],
                                            start=(o == 0), stop=(o == KC - 1))
                    ins.then_inc(w_used, 1)
                elif u[0] == "w1":
                    _, l, k = u
                    for f in range(FC):
                        ins = pe.matmul(streams[1].bank[:, 0, l * FC + f:l * FC + f + 1], raw[:, f * P:(f + 1) * P],
                                        col[:, C_BETA1 + l * KC + k:C_BETA1 + l * KC + k + 1],
                                        start=(l == 0 and k == 0 and f == 0), stop=(k == KC - 1), skip_group_check=True)
                    ins.then_inc(w_used, 1)

        def prep_gpsimd(pool):
            pool.memset(ident[:, :], 0.0).then_inc(ones_ready, 1)
            pool.memset(eye[:, :], 0.0).then_inc(ones_ready, 1)
            pool.wait_ge(ones_ready, 2)
            pool.affine_select(out=ident[:, :], in_=ident[:, :], compare_op=ALU.not_equal, fill=1.0, base=0,
                               pattern=[[-1, P]], channel_multiplier=1).then_inc(ident_ready, 1)
            pool.affine_select(out=eye[:, :], in_=eye[:, :], compare_op=ALU.not_equal, fill=1.0, base=0,
                               pattern=[[-1, N]], channel_multiplier=1).then_inc(ident_ready, 1)
            pool.wait_ge(ident_ready, 2)
            pool.affine_select(out=eye[:, :], in_=eye[:, :], compare_op=ALU.not_equal, fill=1.0, base=-N,
                               pattern=[[-1, N]], channel_multiplier=1).then_inc(ident_ready, 1)
            pool.wait_ge(ident_ready, 3)

        XT = (0, 1)

        def pe_xt(pe, q, g, n, src, z):
            for t in range(TILES):
                if z is not None:
                    pe.wait_ge(*q.sig["z"].at(g, TILES * z + t + 1))
                for k in range(KC):
                    ins = pe.transpose(q.bank[:, XT[k], t * P:(t + 1) * P], src[:, t, k * P:(k + 1) * P], ident[:, :])
                    if t == TILES - 1:
                        ins.then_inc(q.sig["xt_ps"].sem, 1)

        def act_xt(act, q, g, n):
            for k in range(KC):
                yield
                act.wait_ge(*q.sig["xt_ps"].at(g, KC * n + k + 1))
                act.activation(q.xt_h[:, k, :], q.bank[:, XT[k], 0:R], ACT.Copy).then_inc(q.sig["xt_hi"].sem, 1)

        def dve_xt(dve, q, g, n):
            for k in range(KC):
                yield
                dve.wait_ge(*q.sig["xt_hi"].at(g, KC * n + k + 1))
                dve.tensor_tensor(q.xt_l[:, k, :], q.bank[:, XT[k], 0:R], f32(q.xt_h[:, k, :]), ALU.subtract).then_inc(q.sig["xt_lo"].sem, 1)

        def pe_wait_xt(pe, q, g, n):
            pe.wait_ge(*q.sig["xt_lo"].at(g, KC * (n + 1)))

        def pe_rows(pe, q, bank, w):
            for t in range(TILES):
                for k in range(KC):
                    ins = split3(pe, q.bank[:, bank, t * D:(t + 1) * D], q.xt_h[:, k, t * P:(t + 1) * P], q.xt_l[:, k, t * P:(t + 1) * P],
                                 ws_h[:, w, k, :], ws_l[:, w, k, :], k == 0, k == KC - 1)
            return ins

        def pe_cols(pe, q, bank, w):
            for o in range(KC):
                for k in range(KC):
                    ins = split3(pe, q.bank[:, bank, o * R:(o + 1) * R], ws_h[:, w, k, o * P:(o + 1) * P], ws_l[:, w, k, o * P:(o + 1) * P],
                                 q.xt_h[:, k, :], q.xt_l[:, k, :], k == 0, k == KC - 1)
            return ins

        def pe_rep(pe, q):
            for k in range(KC):
                ins = split3(pe, q.bank[:, 1, 0:R], rep_h[:, k, :], rep_l[:, k, :], q.xt_h[:, k, :], q.xt_l[:, k, :], k == 0, k == KC - 1)
            ins.then_inc(q.sig["lin_ps"].sem, 1)

        def dve_norm(dve, q, g, n, dst):
            dve.wait_ge(*q.sig["u"].at(g, n + 1))
            for t in range(TILES):
                dve.bn_stats(q.stat[:, t, :], q.u_sb[:, t, :]).then_inc(q.sig["st"].sem, 1)
            yield
            for t in range(TILES):
                dve.wait_ge(*q.sig["st"].at(g, TILES * n + t + 1))
                dve.sem_inc(gate["dve"], 1)
                dve.bn_aggr(q.mv_sb[:, t, :], q.stat[:, t, :]).then_inc(q.sig["mv"].sem, 1)
            dve.wait_ge(*q.sig["mv"].at(g, TILES * (n + 1)))
            dve.tensor_scalar(q.ve_sb[:, :], q.mv_sb[:, :, 1], EPS, None, ALU.add).then_inc(q.sig["ve"].sem, 1)
            yield
            dve.wait_ge(*q.sig["rstd"].at(g, n + 1))
            for t in range(TILES):
                dve.tensor_scalar(dst[:, t, :], q.u_sb[:, t, :], q.mv_sb[:, t, 0:1], q.rstd_sb[:, t:t + 1],
                                  ALU.subtract, ALU.mult).then_inc(q.sig["z"].sem, 1)

        def pool_norm(pool, q, g, n):
            yield
            pool.wait_ge(*q.sig["ve"].at(g, n + 1))
            pool.tensor_tensor(q.rstd_sb[:, :], q.ve_sb[:, :], mhalf[:, :], ALU.pow).then_inc(q.sig["rstd"].sem, 1)

        def pool_affine(pool, q, g, l, dst, gain, bias, done):
            pool.tensor_tensor(dst[:, :, :], q.u_sb[:, :, :], row[:, gain + l:gain + l + 1, :].to_broadcast([P, TILES, D]), ALU.mult).then_inc(q.sig[done].sem, 1)
            pool.wait_ge(*q.sig[done].at(g, 2 * l + 1))
            pool.tensor_tensor(dst[:, :, :], dst[:, :, :], row[:, bias + l:bias + l + 1, :].to_broadcast([P, TILES, D]), ALU.add).then_inc(q.sig[done].sem, 1)

        def dve_leaky_max(dve, q, g, n):
            dve.scalar_tensor_tensor(out=q.scores[:, :, :], in0=q.scores[:, :, :], scalar=0.2, in1=q.scores[:, :, :],
                                     op0=ALU.mult, op1=ALU.max).then_inc(q.sig["leak"].sem, 1)
            yield
            dve.wait_ge(*q.sig["leak"].at(g, n + 1))
            dve.tensor_reduce(q.mx[:, 0:TILES], q.scores[:, :, :], AX_X, ALU.max, negate=True).then_inc(q.sig["e_max"].sem, 1)

        def dve_mask_max(dve, q, g, n, scores, neg):
            dve.tensor_tensor(q.scores[:, :, :], scores, neg, ALU.add).then_inc(q.sig["e_add"].sem, 1)
            yield
            dve.wait_ge(*q.sig["e_add"].at(g, 2))
            dve.tensor_reduce(q.mx[:, 0:TILES], q.scores[:, :, :], AX_X, ALU.max, negate=True).then_inc(q.sig["e_max"].sem, 1)

        def act_exp(act, q, g, n):
            act.wait_ge(*q.sig["e_max"].at(g, n + 1))
            for t in range(TILES):
                act.activation(q.scores[:, t, :], q.scores[:, t, :], ACT.Exp, bias=q.mx[:, t:t + 1],
                               accum_out=q.sm[:, t:t + 1]).then_inc(q.sig["e_exp"].sem, 1)

        def dve_inv(dve, q, g, n):
            dve.wait_ge(*q.sig["e_exp"].at(g, TILES * (n + 1)))
            dve.reciprocal(q.sm[:, 0:TILES], q.sm[:, 0:TILES]).then_inc(q.sig["e_inv"].sem, 1)

        def pe_pt(pe, q, g, n, bank):
            for t in range(TILES):
                pe.wait_ge(*q.sig["e_exp"].at(g, TILES * n + t + 1))
                ins = pe.transpose(q.bank[:, bank, t * P:(t + 1) * P], q.scores[:, t, :], ident[:, :])
            ins.then_inc(q.sig["pt_ps"].sem, 1)

        def act_pt(act, q, g, n, bank):
            act.wait_ge(*q.sig["pt_ps"].at(g, n))
            act.activation(q.pt[:, 0:TILES * P], q.bank[:, bank, 0:TILES * P], ACT.Copy).then_inc(q.sig["pt_sb"].sem, 1)

        def pe_agg(pe, q, banks, lhs, rhs):
            for t in range(TILES):
                pe.matmul(q.bank[:, banks[t], t * D:(t + 1) * D], lhs[:, t * P:(t + 1) * P], rhs[:, t, :], start=True, stop=True).then_inc(q.sig["agg_ps"].sem, 1)

        def l0_tensor(pe, q, g):
            yield
            pe.wait_ge(*q.sig["load"].at(g, 32))
            pe_xt(pe, q, g, 0, q.xin, None)
            yield
            pe_wait_xt(pe, q, g, 0)
            pe_rows(pe, q, 3, WV).then_inc(q.sig["qkv_ps"].sem, 1)
            yield
            pe_cols(pe, q, 1, WQ).then_inc(q.sig["qkv_ps"].sem, 1)
            yield
            pe_cols(pe, q, 2, WK).then_inc(q.sig["qkv_ps"].sem, 1)
            yield
            pe.wait_ge(*q.sig["qk_sb"].at(g, 2))
            pe.wait_ge(*q.sig["vsw_sb"].at(g, 2))
            for t in range(TILES):
                if t:
                    yield
                for hc in range(HC):
                    for b in range(2):
                        for r in range(RG):
                            c = (t * HC + hc) * N
                            rows_ = slice(t * P + b * N, t * P + (b + 1) * N)
                            ins = pe.matmul(q.bank[b * N:(b + 1) * N, r, c:c + N], q.work[r * DK:(r + 1) * DK, hc, rows_],
                                            q.work[r * DK:(r + 1) * DK, HC + hc, rows_], start=True, stop=True)
            ins.then_inc(q.sig["s_ps"].sem, 1)
            for t in range(TILES):
                yield
                pe.wait_ge(*q.sig["p_norm"].at(g, t + 1))
                pe.wait_ge(*q.sig["p_add"].at(g, 2))
                for r in range(RG):
                    ins = pe.transpose(q.bank[:, t, r * P:(r + 1) * P], q.work[:, 2 * t + r // 2, (r % 2) * P:(r % 2 + 1) * P], ident[:, :])
                ins.then_inc(q.sig["pt0_ps"].sem, 1)
                yield
                pe.wait_ge(*q.sig["pt0_sb"].at(g, t + 1))
                pe.sem_inc(gate["pe"], 1)
                for r in range(RG):
                    for b in range(2):
                        for hc in range(HC):
                            v = q.val if b == hc else q.val_sw
                            h = hc * RG + r
                            ins = pe.matmul(q.bank[r * DK:(r + 1) * DK, 2 + hc, t * P + b * N:t * P + (b + 1) * N],
                                            v[hc * N:(hc + 1) * N, t, h * DK:(h + 1) * DK],
                                            q.pt[hc * N:(hc + 1) * N, r * P + b * N:r * P + (b + 1) * N], start=True, stop=True)
                ins.then_inc(q.sig["pv0_ps"].sem, 1)
            yield
            pe.wait_ge(*q.sig["o_lo"].at(g, 2))
            pe_rows(pe, q, 0, WO).then_inc(q.sig["y_ps"].sem, 1)

        def l0_scalar(act, q, g):
            yield from act_xt(act, q, g, 0)
            yield
            act.wait_ge(*q.sig["qkv_ps"].at(g, 1))
            act.activation(q.val[:, :, :].rearrange("p t d -> p (t d)"), q.bank[:, 3, :], ACT.Copy).then_inc(q.sig["v_sb"].sem, 1)
            yield
            act.wait_ge(*q.sig["qkv_ps"].at(g, 2))
            act.activation(q.work[:, 0:HC, :].rearrange("p c r -> p (c r)"), q.bank[:, 1, :], ACT.Copy, scale=DK ** -0.5).then_inc(q.sig["qk_sb"].sem, 1)
            yield
            act.wait_ge(*q.sig["qkv_ps"].at(g, 3))
            act.activation(q.work[:, HC:2 * HC, :].rearrange("p c r -> p (c r)"), q.bank[:, 2, :], ACT.Copy).then_inc(q.sig["qk_sb"].sem, 1)
            yield
            act.wait_ge(*q.sig["p_sub"].at(g, 1))
            p = q.work[:, 0:2, :].rearrange("p c r -> p (c r)")
            act.activation(p, p, ACT.Exp).then_inc(q.sig["p_exp"].sem, 1)
            yield
            act.wait_ge(*q.sig["p_sub"].at(g, 2))
            p = q.work[:, 2:4, :].rearrange("p c r -> p (c r)")
            act.activation(p, p, ACT.Exp).then_inc(q.sig["p_exp"].sem, 1)
            for t in range(TILES):
                yield
                act.wait_ge(*q.sig["pt0_ps"].at(g, t + 1))
                if t:
                    act.wait_ge(*q.sig["pv0_ps"].at(g, t))
                act.activation(q.pt[:, :], q.bank[:, t, :], ACT.Copy).then_inc(q.sig["pt0_sb"].sem, 1)
            for k in range(KC):
                yield
                act.wait_ge(*q.sig["pv0_ps"].at(g, 2))
                act.activation(q.xt_h[:, k, :], q.bank[:, 2 + k, 0:R], ACT.Relu).then_inc(q.sig["o_hi"].sem, 1)

        def l0_vector(dve, q, g):
            yield from dve_xt(dve, q, g, 0)
            yield
            dve.wait_ge(*q.sig["qkv_ps"].at(g, 1))
            dve.wait_ge(*q.sig["v_sb"].at(g, 1))
            for b in range(2):
                dve.tensor_copy(q.val_sw[(1 - b) * N:(2 - b) * N, :, :].rearrange("p t d -> p (t d)"), q.bank[b * N:(b + 1) * N, 3, :]).then_inc(q.sig["vsw_sb"].sem, 1)

            def softmax_front(t):
                yield
                dve.wait_ge(*q.sig["s_ps"].at(g, 1))
                dve.wait_ge(*q.sig["mask"].at(g, 1))
                p4 = q.work[:, 2 * t:2 * t + 2, :].rearrange("p c (r h j) -> p (c r) h j", r=2, h=HC)
                p = q.work[:, 2 * t:2 * t + 2, :].rearrange("p c (h j) -> p (c h) j", j=N)
                m = q.mx[:, t * NH:(t + 1) * NH]
                dve.tensor_tensor(p4, q.bank[:, :, t * HC * N:(t + 1) * HC * N].rearrange("p r (h j) -> p r h j", h=HC),
                                  q.negc[:, t:t + 1, :].unsqueeze(1).to_broadcast([P, RG, HC, N]), ALU.add).then_inc(q.sig["p_add"].sem, 1)
                yield
                dve.wait_ge(*q.sig["p_add"].at(g, t + 1))
                dve.tensor_reduce(m, p, AX_X, ALU.max).then_inc(q.sig["p_max"].sem, 1)
                yield
                dve.wait_ge(*q.sig["p_max"].at(g, t + 1))
                dve.tensor_tensor(p, p, m.unsqueeze(2).to_broadcast([P, NH, N]), ALU.subtract).then_inc(q.sig["p_sub"].sem, 1)

            def softmax_back(t):
                yield
                p = q.work[:, 2 * t:2 * t + 2, :].rearrange("p c (h j) -> p (c h) j", j=N)
                sm = q.sm[:, t * NH:(t + 1) * NH]
                dve.wait_ge(*q.sig["p_exp"].at(g, t + 1))
                dve.tensor_reduce(sm, p, AX_X, ALU.add).then_inc(q.sig["p_div"].sem, 1)
                yield
                dve.wait_ge(*q.sig["p_div"].at(g, 2 * t + 1))
                dve.reciprocal(sm, sm).then_inc(q.sig["p_div"].sem, 1)
                dve.wait_ge(*q.sig["p_div"].at(g, 2 * t + 2))
                dve.tensor_tensor(p, p, sm.unsqueeze(2).to_broadcast([P, NH, N]), ALU.mult).then_inc(q.sig["p_norm"].sem, 1)

            yield from softmax_front(0)
            yield from softmax_front(1)
            yield from softmax_back(0)
            yield from softmax_back(1)
            for k in range(KC):
                yield
                dve.wait_ge(*q.sig["o_hi"].at(g, k + 1))
                dve.scalar_tensor_tensor(out=q.xt_l[:, k, :], in0=q.bank[:, 2 + k, 0:R], scalar=0.0, in1=f32(q.xt_h[:, k, :]),
                                         op0=ALU.max, op1=ALU.subtract).then_inc(q.sig["o_lo"].sem, 1)
            yield
            dve.wait_ge(*q.sig["y_ps"].at(g, 1))
            dve.wait_ge(q.sig["out"].sem, 16 * g + 1)
            dve.tensor_tensor(q.u_sb[:, :, :], q.xin[:, :, :], q.bank[:, 0, :].rearrange("p (t d) -> p t d", t=TILES), ALU.add).then_inc(q.sig["u"].sem, 1)
            yield
            yield from dve_norm(dve, q, g, 0, q.xrow)

        def l0_gpsimd(pool, q, g):
            yield
            pool.wait_ge(*q.sig["load"].at(g, 32))
            pool.sem_inc(gate["pool"], 1)
            pool.tensor_copy(q.adjf_sb[:, :, :], q.adji[:, :, :]).then_inc(q.sig["adjf"].sem, 1)
            pool.wait_ge(*q.sig["adjf"].at(g, 1))
            pool.sem_inc(gate["pool"], 1)
            pool.tensor_scalar(q.negc[:, :, :], q.adjf_sb[:, :, :], 0.0, MASKED, ALU.is_equal, ALU.mult).then_inc(q.sig["mask"].sem, 1)
            pool.tensor_scalar(q.negm[:, :, 0:N], q.adjf_sb[:, :, :], 0.0, MASKED, ALU.is_equal, ALU.mult).then_inc(q.sig["mask"].sem, 1)
            pool.wait_ge(*q.sig["mask"].at(g, 2))
            pool.sem_inc(gate["pool"], 1)
            pool_spread(pool, q, q.negm)
            yield from pool_norm(pool, q, g, 0)

        def pool_spread(pool, q, neg):
            for b in (1, 0):
                pool.tensor_scalar(neg[:, :, b * N:(b + 1) * N], neg[:, :, 0:N], other[:, b:b + 1], None, ALU.add).then_inc(q.sig["mask"].sem, 1)

        def l1_tensor(pe, q, g):
            yield
            pe_xt(pe, q, g, 1, q.xrow, 0)
            yield
            pe_wait_xt(pe, q, g, 1)
            pe_rows(pe, q, 2, W1H).then_inc(q.sig["wh_ps"].sem, 1)
            yield
            pe_rep(pe, q)
            yield
            pe.wait_ge(*q.sig["mask"].at(g, 7))
            for t in range(TILES):
                ins = pe.transpose(q.bank[:, 3, t * P:(t + 1) * P], q.neg1[:, t, :], ident[:, :])
            ins.then_inc(q.sig["negt_ps"].sem, 1)
            yield
            pe.wait_ge(*q.sig["e_norm"].at(g, 2))
            pe_agg(pe, q, (0, 0), q.scores[:, :, :].rearrange("p t j -> p (t j)"), q.val)

        def l1_scalar(act, q, g):
            yield from act_xt(act, q, g, 1)
            yield
            act.wait_ge(*q.sig["wh_ps"].at(g, 1))
            act.activation(q.val[:, :, :].rearrange("p t d -> p (t d)"), q.bank[:, 2, :], ACT.Copy).then_inc(q.sig["wh_sb"].sem, 1)
            yield
            act.wait_ge(*q.sig["lin_ps"].at(g, 1))
            for t in range(TILES):
                act.wait_ge(*q.sig["sc_dot"].at(g, t + 1))
                act.activation(q.scores[:, t, :], q.bank[:, 1, t * P:(t + 1) * P], ACT.Identity, bias=q.sc[:, t:t + 1]).then_inc(q.sig["lin"].sem, 1)
            yield
            act_exp(act, q, g, 0)
            yield
            act.wait_ge(*q.sig["agg_ps"].at(g, 2))
            act.activation(q.u_sb[:, :, :].rearrange("p t d -> p (t d)"), q.bank[:, 0, :], ACT.Copy).then_inc(q.sig["h1_sb"].sem, 1)

        def l1_vector(dve, q, g):
            yield from dve_xt(dve, q, g, 1)
            yield
            dve.wait_ge(*q.sig["wh_sb"].at(g, 1))
            for t in range(TILES):
                dve.tensor_tensor_reduce(out=q.val_sw[:, t, :], in0=q.val[:, t, :], in1=row[:, R_A2, :], scale=1.0, scalar=0.0,
                                         op0=ALU.mult, op1=ALU.add, accum_out=q.sc[:, t:t + 1]).then_inc(q.sig["sc_dot"].sem, 1)
            yield
            dve.wait_ge(*q.sig["lin"].at(g, TILES))
            dve.wait_ge(*q.sig["negt_ps"].at(g, 1))
            dve.tensor_tensor(q.scores[:, :, :], q.scores[:, :, :], q.bank[:, 3, 0:TILES * P].rearrange("p (t j) -> p t j", t=TILES),
                              ALU.add).then_inc(q.sig["e_add"].sem, 1)
            yield
            dve.wait_ge(*q.sig["e_add"].at(g, 1))
            yield from dve_leaky_max(dve, q, g, 0)
            yield
            dve_inv(dve, q, g, 0)
            dve.wait_ge(*q.sig["e_inv"].at(g, 1))
            for t in range(TILES):
                dve.tensor_scalar(q.scores[:, t, :], q.scores[:, t, :], q.sm[:, t:t + 1], None, ALU.mult).then_inc(q.sig["e_norm"].sem, 1)
            yield
            dve.wait_ge(*q.sig["h1_sb"].at(g, 1))
            dve.scalar_tensor_tensor(out=q.u_sb[:, :, :], in0=q.u_sb[:, :, :], scalar=0.2, in1=q.u_sb[:, :, :],
                                     op0=ALU.mult, op1=ALU.max).then_inc(q.sig["leaky"].sem, 1)
            yield
            dve.wait_ge(*q.sig["leaky"].at(g, 1))
            dve.tensor_tensor(q.u_sb[:, :, :], q.u_sb[:, :, :], q.xrow[:, :, :], ALU.add).then_inc(q.sig["u"].sem, 1)
            yield
            yield from dve_norm(dve, q, g, 1, q.xrow)

        def l1_gpsimd(pool, q, g):
            yield
            pool.wait_ge(*q.sig["z"].at(g, TILES))
            pool.sem_inc(gate["pool"], 1)
            pool.tensor_scalar(q.neg1[:, :, 0:N], q.adjf_sb[:, :, :], 0.0, MASKED_L1, ALU.is_le, ALU.mult).then_inc(q.sig["mask"].sem, 1)
            pool.wait_ge(*q.sig["mask"].at(g, 5))
            pool.sem_inc(gate["pool"], 1)
            pool_spread(pool, q, q.neg1)
            yield from pool_norm(pool, q, g, 1)

        def l2_tensor(pe, q, g):
            yield
            pe_xt(pe, q, g, 2, q.xrow, 1)
            yield
            pe_wait_xt(pe, q, g, 2)
            pe_cols(pe, q, 1, W2T).then_inc(q.sig["h_ps"].sem, 1)
            yield
            pe_cols(pe, q, 2, W2M).then_inc(q.sig["h_ps"].sem, 1)
            yield
            pe_rows(pe, q, 3, W2T).then_inc(q.sig["h_ps"].sem, 1)
            yield
            pe.wait_ge(*q.sig["h_sb"].at(g, 2))
            pe.wait_ge(*q.sig["ha_sb"].at(g, 2))
            for t in range(TILES):
                for k in range(KC):
                    ins = pe.matmul(q.bank[:, 0, t * P:(t + 1) * P], q.work[:, KC + k, t * P:(t + 1) * P], q.work[:, k, t * P:(t + 1) * P],
                                    start=(k == 0), stop=(k == KC - 1))
            ins.then_inc(q.sig["sc_ps"].sem, 1)
            yield
            pe_pt(pe, q, g, 1, 1)
            yield
            pe.wait_ge(*q.sig["pt_sb"].at(g, 1))
            pe.wait_ge(*q.sig["hrow_sb"].at(g, 1))
            pe_agg(pe, q, (2, 2), q.pt, q.val)

        def l2_scalar(act, q, g):
            yield from act_xt(act, q, g, 2)
            yield
            act.wait_ge(*q.sig["h_ps"].at(g, 1))
            for o in range(KC):
                act.activation(q.work[:, o, :], q.bank[:, 1, o * R:(o + 1) * R], ACT.Identity, bias=col[:, C_LB + o:C_LB + o + 1]).then_inc(q.sig["h_sb"].sem, 1)
            yield
            act_exp(act, q, g, 1)
            yield
            act_pt(act, q, g, 1, 1)
            yield
            act.wait_ge(*q.sig["elu_m"].at(g, 1))
            m = q.work[:, 0:TILES, :]
            act.activation(m, m, ACT.Exp).then_inc(q.sig["elu_e"].sem, 1)

        def l2_vector(dve, q, g):
            yield from dve_xt(dve, q, g, 2)
            yield
            dve.wait_ge(*q.sig["h_ps"].at(g, 2))
            for o in range(KC):
                dve.tensor_scalar(q.work[:, KC + o, :], q.bank[:, 2, o * R:(o + 1) * R], mcol[:, o:o + 1], None, ALU.add).then_inc(q.sig["ha_sb"].sem, 1)
            yield
            dve.wait_ge(*q.sig["h_ps"].at(g, 3))
            dve.tensor_tensor(q.val[:, :, :], q.bank[:, 3, :].rearrange("p (t d) -> p t d", t=TILES),
                              row[:, R_LB:R_LB + 1, :].to_broadcast([P, TILES, D]), ALU.add).then_inc(q.sig["hrow_sb"].sem, 1)
            yield
            dve.wait_ge(*q.sig["sc_ps"].at(g, 1))
            dve.wait_ge(*q.sig["mask"].at(g, 4))
            yield from dve_mask_max(dve, q, g, 1, q.bank[:, 0, 0:TILES * P].rearrange("p (t j) -> p t j", t=TILES), q.negm[:, :, :])
            yield
            dve_inv(dve, q, g, 1)
            yield
            dve.wait_ge(*q.sig["agg_ps"].at(g, 4))
            dve.wait_ge(*q.sig["e_inv"].at(g, 2))
            for t in range(TILES):
                dve.tensor_scalar(q.u_sb[:, t, :], q.bank[:, 2, t * D:(t + 1) * D], q.sm[:, t:t + 1], None, ALU.mult).then_inc(q.sig["elu"].sem, 1)
            yield
            dve.wait_ge(*q.sig["elu"].at(g, 2))
            dve.tensor_scalar(q.work[:, 0:TILES, :], q.u_sb[:, :, :], 0.0, None, ALU.min).then_inc(q.sig["elu_m"].sem, 1)
            yield
            dve.wait_ge(*q.sig["elu_e"].at(g, 1))
            dve.scalar_tensor_tensor(out=q.u_sb[:, :, :], in0=q.u_sb[:, :, :], scalar=0.0, in1=q.work[:, 0:TILES, :],
                                     op0=ALU.max, op1=ALU.add).then_inc(q.sig["elu"].sem, 1)
            yield
            dve.wait_ge(*q.sig["elu"].at(g, 3))
            dve.scalar_tensor_tensor(out=q.u_sb[:, :, :], in0=q.u_sb[:, :, :], scalar=-1.0, in1=q.xrow[:, :, :],
                                     op0=ALU.add, op1=ALU.add).then_inc(q.sig["u"].sem, 1)
            yield
            yield from dve_norm(dve, q, g, 2, q.xkeep)

        def l2_gpsimd(pool, q, g):
            yield
            pool.wait_ge(*q.sig["e_add"].at(g, 2))
            pool.tensor_tensor(q.adjf_sb[:, :, :], q.adjf_sb[:, :, :], eye[:, :].unsqueeze(1).to_broadcast([P, TILES, N]), ALU.add).then_inc(q.sig["mask"].sem, 1)
            pool.wait_ge(*q.sig["mask"].at(g, 8))
            pool.sem_inc(gate["pool"], 1)
            pool.tensor_scalar(q.negm[:, :, 0:N], q.adjf_sb[:, :, :], 0.0, MASKED, ALU.is_le, ALU.mult).then_inc(q.sig["mask"].sem, 1)
            pool.wait_ge(*q.sig["mask"].at(g, 9))
            pool.sem_inc(gate["pool"], 1)
            pool_spread(pool, q, q.negm)
            yield from pool_norm(pool, q, g, 2)

        def at_tensor(pe, q, g, l):
            yield
            pe.wait_ge(*q.sig["sc_dot"].at(g, TILES * (2 + 2 * l)))
            for t in range(TILES):
                ins = pe.matmul(q.bank[:, 1, t * P:(t + 1) * P], q.sj[:, t:t + 1].to_broadcast([P, P]), ident[:, :], start=True, stop=True)
            ins.then_inc(q.sig["lin_ps"].sem, 1)
            yield
            pe_pt(pe, q, g, 2 + l, 2)
            yield
            pe.wait_ge(*q.sig["pt_sb"].at(g, 2 + l))
            if l:
                pe.wait_ge(*q.sig["aff"].at(g, 2 * l))
            pe_agg(pe, q, (3, 0), q.pt, q.xrow if l else q.xkeep)

        def at_scalar(act, q, g, l):
            yield
            act_exp(act, q, g, 2 + l)
            yield
            act_pt(act, q, g, 2 + l, 2)

        def at_vector(dve, q, g, l):
            src = q.u_sb if l else q.xkeep
            yield
            dve.wait_ge(*q.sig["z"].at(g, TILES * (3 + 2 * l)))
            for r, parts, junk in ((R_WJ, q.sj, q.val), (R_WI, q.sc, q.val_sw)):
                for t in range(TILES):
                    dve.tensor_tensor_reduce(out=junk[:, t, :], in0=src[:, t, :], in1=row[:, r + l, :], scale=1.0, scalar=0.0,
                                             op0=ALU.mult, op1=ALU.add, accum_out=parts[:, t:t + 1]).then_inc(q.sig["sc_dot"].sem, 1)
                yield
            dve.wait_ge(*q.sig["sc_dot"].at(g, TILES * (3 + 2 * l)))
            dve.tensor_scalar(q.sc[:, :], q.sc[:, :], abias[:, l:l + 1], None, ALU.add).then_inc(q.sig["sc_ready"].sem, 1)
            yield
            dve.wait_ge(*q.sig["lin_ps"].at(g, 2 + l))
            dve.wait_ge(*q.sig["sc_ready"].at(g, 1 + l))
            if l == 0:
                dve.wait_ge(*q.sig["mask"].at(g, 11))
            for t in range(TILES):
                dve.scalar_tensor_tensor(out=q.scores[:, t, :], in0=q.bank[:, 1, t * P:(t + 1) * P], scalar=q.sc[:, t:t + 1], in1=q.negm[:, t, :],
                                         op0=ALU.add, op1=ALU.add).then_inc(q.sig["lin"].sem, 1)
            yield
            dve.wait_ge(*q.sig["lin"].at(g, TILES * (2 + l)))
            yield from dve_leaky_max(dve, q, g, 1 + l)
            yield
            dve_inv(dve, q, g, 2 + l)
            rows_ = q.xrow if l else q.xkeep
            for t in range(TILES):
                yield
                dve.wait_ge(*q.sig["agg_ps"].at(g, TILES * (2 + l) + t + 1))
                dve.wait_ge(*q.sig["e_inv"].at(g, 3 + l))
                dve.scalar_tensor_tensor(out=q.u_sb[:, t, :], in0=q.bank[:, 3 - 3 * t, t * D:(t + 1) * D], scalar=q.sm[:, t:t + 1], in1=rows_[:, t, :],
                                         op0=ALU.mult, op1=ALU.add).then_inc(q.sig["u" if t else "u_b"].sem, 1)
            yield
            dve.wait_ge(*q.sig["u_b"].at(g, 1 + l))
            yield from dve_norm(dve, q, g, 3 + 2 * l, q.u_sb)

        def at_gpsimd(pool, q, g, l):
            yield
            if l:
                pool.wait_ge(*q.sig["z"].at(g, TILES * (3 + 2 * l)))
                pool_affine(pool, q, g, l - 1, q.xrow, R_G2, R_B2, "aff")
            yield from pool_norm(pool, q, g, 3 + 2 * l)

        LAGC = 3

        F_BANKS = (1, 2, 0)

        def ff_tensor(pe, q, g, l):
            yield
            pe_xt(pe, q, g, 3 + l, q.u_sb, 3 + 2 * l)
            for f in range(FC + LAGC):
                if f < FC:
                    yield
                    if f == 0:
                        pe_wait_xt(pe, q, g, 3 + l)
                    if f >= 3:
                        pe.wait_ge(*q.sig["ff_gelu"].at(g, l * FC + f - 2))
                    for k in range(KC):
                        ins = split3(pe, q.bank[:, F_BANKS[f % 3], 0:R], w1_h[:, l, k, f * P:(f + 1) * P], w1_l[:, l, k, f * P:(f + 1) * P],
                                     q.xt_h[:, k, :], q.xt_l[:, k, :], k == 0, k == KC - 1)
                    ins.then_inc(q.sig["f_ps"].sem, 1)
                if f >= LAGC:
                    c = f - LAGC
                    yield
                    pe.wait_ge(*q.sig["ff_lo"].at(g, l * FC + c + 1))
                    for t in range(TILES):
                        ins = split3(pe, q.bank[:, 3, t * D:(t + 1) * D], q.g_hi[:, c % 2, t * P:(t + 1) * P], q.g_lo[:, c % 2, t * P:(t + 1) * P],
                                     w2_h[:, l, c, :], w2_l[:, l, c, :], c == 0, c == FC - 1, start=(t == 0))
                    ins.then_inc(q.sig["ff_used"].sem, 1)

        def ff_scalar(act, q, g, l):
            yield from act_xt(act, q, g, 3 + l)
            for f in range(FC):
                yield
                act.wait_ge(*q.sig["f_ps"].at(g, l * FC + f + 1))
                if f >= 4:
                    act.wait_ge(*q.sig["ff_lo"].at(g, l * FC + f - 3))
                act.activation(q.work[:, f % 4, :], q.bank[:, F_BANKS[f % 3], 0:R], ACT.Gelu, bias=ffb[:, l * FC + f:l * FC + f + 1]).then_inc(q.sig["ff_gelu"].sem, 1)
                yield
                if f >= 2:
                    act.wait_ge(*q.sig["ff_used"].at(g, l * FC + f - 1))
                act.wait_ge(*q.sig["ff_gelu"].at(g, l * FC + f + 1))
                act.activation(q.g_hi[:, f % 2, :], q.work[:, f % 4, :], ACT.Copy).then_inc(q.sig["ff_hi"].sem, 1)

        def ff_vector(dve, q, g, l):
            yield from dve_xt(dve, q, g, 3 + l)
            for f in range(FC):
                yield
                dve.wait_ge(*q.sig["ff_hi"].at(g, l * FC + f + 1))
                dve.tensor_tensor(q.g_lo[:, f % 2, :], q.work[:, f % 4, :], f32(q.g_hi[:, f % 2, :]), ALU.subtract).then_inc(q.sig["ff_lo"].sem, 1)
            yield
            dve.wait_ge(*q.sig["ff_used"].at(g, (l + 1) * FC))
            dve.wait_ge(*q.sig["hb"].at(g, 2 * l + 2))
            dve.tensor_tensor(q.u_sb[:, :, :], q.val_sw[:, :, :], q.bank[:, 3, :].rearrange("p (t d) -> p t d", t=TILES), ALU.add).then_inc(q.sig["u"].sem, 1)
            if l < L - 1:
                yield
                yield from dve_norm(dve, q, g, 4 + 2 * l, q.u_sb)

        def tail_vector(dve, q, g):
            yield
            yield from dve_norm(dve, q, g, 2 * L + 2, q.u_sb)
            yield
            dve.wait_ge(*q.sig["aff"].at(g, 2 * L))
            dve.tensor_tensor(q.u_sb[:, :, :], q.xrow[:, :, :], q.xkeep[:, :, :], ALU.add).then_inc(q.sig["u"].sem, 1)
            yield
            yield from dve_norm(dve, q, g, 2 * L + 3, q.xrow)

        def ff_gpsimd(pool, q, g, l):
            yield
            pool.wait_ge(*q.sig["z"].at(g, TILES * (4 + 2 * l)))
            pool_affine(pool, q, g, l, q.val_sw, R_G1, R_B1, "hb")
            if l < L - 1:
                yield from pool_norm(pool, q, g, 4 + 2 * l)

        def tail_gpsimd(pool, q, g):
            yield from pool_norm(pool, q, g, 2 * L + 2)
            yield
            pool.wait_ge(*q.sig["z"].at(g, TILES * (2 * L + 3)))
            pool_affine(pool, q, g, L - 1, q.xrow, R_G2, R_B2, "aff")
            yield from pool_norm(pool, q, g, 2 * L + 3)

        def sync_out(sp, q, g):
            yield
            sp.wait_ge(*q.sig["z"].at(g, 10 * TILES))
            sp.sem_inc(gate["sp"], 1)
            sp.dma_start(out_v[2 * g + q.s], q.xrow[:, :, :]).then_inc(q.sig["out"].sem, 16)

        def sync_load(sp, q, g):
            sp.dma_start(q.xin[:, :, :], x_v[2 * g + q.s]).then_inc(q.sig["load"].sem, 16)
            sp.dma_start(q.adji[:, :, :], adj_v[2 * g + q.s]).then_inc(q.sig["load"].sem, 16)

        STEPS = {
            "tensor": (l0_tensor, l1_tensor, l2_tensor, at_tensor, ff_tensor),
            "scalar": (l0_scalar, l1_scalar, l2_scalar, at_scalar, ff_scalar),
            "vector": (l0_vector, l1_vector, l2_vector, at_vector, ff_vector),
            "gpsimd": (l0_gpsimd, l1_gpsimd, l2_gpsimd, at_gpsimd, ff_gpsimd),
        }

        DUE = {
            "tensor": (
                (-10.02, 1.72, 12.79, 18.18, 26.13, 31.37, 51.84, 58.77, 66.03, 75.28, 83.62,),
                (8.74, 17.77, 21.62, 22.22, 26.94,),
                (9.07, 14.17, 21.40, 21.42, 26.66, 34.58, 38.35,),
                (1.66, 13.31, 17.03,),
                (12.28, 19.42, 19.88, 22.86, 23.81, 25.63, 33.26, 33.91, 33.93, 33.95, 33.97, 34.98, 35.00, 36.28, 37.15, 39.21, 39.80,),
                (),
            ),
            "scalar": (
                (-7.23, -1.86, 4.81, 22.10, 23.43, 39.21, 53.43, 53.75, 70.95, 75.83, 77.03,),
                (15.98, 16.13, 18.53, 22.93, 23.86, 26.96,),
                (11.02, 11.04, 20.27, 31.91, 35.07, 42.45,),
                (6.70, 14.72,),
                (13.09, 13.46, 20.99, 24.05, 24.07, 24.09, 24.12, 26.68, 27.70, 33.93, 33.95, 33.97, 33.99, 35.00, 35.02, 36.30, 36.32,
                 37.20,),
                (),
            ),
            "vector": (
                (-3.60, -1.77, 10.20, 32.82, 34.59, 36.36, 37.04, 38.37, 40.61, 42.95, 46.54, 53.45, 53.95, 80.13, 80.47, 84.77, 84.79,
                 84.81, 84.85,),
                (16.00, 16.15, 20.58, 23.52, 23.81, 23.84, 25.02, 26.99, 27.51, 29.80, 30.66, 31.69,),
                (11.04, 11.26, 24.66, 25.99, 26.68, 31.67, 36.72, 38.37, 38.65, 46.59, 48.56, 48.58, 49.05, 50.35,),
                (-12.37, 0.74, 1.38, 2.80, 4.48, 4.82, 10.84, 18.61, 18.63, 18.91, 19.11, 19.15,),
                (13.11, 13.79, 24.07, 26.41, 28.27, 33.95, 35.99, 36.85, 37.40, 37.97, 40.51, 40.54, 40.56, 42.53,),
                (5.52, 6.60, 21.26, 31.08, 32.15, 32.36, 61.08,),
            ),
            "gpsimd": (
                (-73.20, 84.83,),
                (-73.49, 30.68,),
                (29.91, 49.17,),
                (-86.48, 19.13,),
                (-87.57, 42.51,),
                (19.51, 21.95, 51.42,),
            ),
            "sync": ((), (), (), (), (0.0,), (0.0,)),
        }
        LEAD = (1, 5)
        START = (
            (296.57, 16.01, 48.51, 104.44, 124.56, 170.69, 192.16, 234.82, 254.24, 317.35),
            (123.54, 208.71, 241.11, 291.52, 311.17, 0.00, 19.36, 63.72, 82.92, 123.54),
        )

        def phase(eng, kind, ph, q, g, more):
            if kind == "sync":
                if ph == PHASES - 3 and more:
                    yield
                    eng.wait_ge(*q.sig["u"].at(g, 1))
                    eng.sem_inc(gate["sp"], 1)
                    eng.wait_ge(*q.sig["adjf"].at(g, 1))
                    eng.sem_inc(gate["sp"], 1)
                    sync_load(eng, q, g + 1)
                if ph == TAIL:
                    yield from sync_out(eng, q, g)
            elif ph == TAIL:
                if kind == "vector":
                    yield from tail_vector(eng, q, g)
                if kind == "gpsimd":
                    yield from tail_gpsimd(eng, q, g)
            elif ph < 3:
                yield from STEPS[kind][ph](eng, q, g)
            elif ph % 2:
                yield from STEPS[kind][3](eng, q, g, (ph - 3) // 2)
            else:
                yield from STEPS[kind][4](eng, q, g, (ph - 4) // 2)

        def run_phases(eng, kind, q, todo):
            for ph, g, more in todo:
                if not isinstance(g, int) and kind != "sync":
                    own = eng.alloc_register(f"{kind}_{q.s}_{ph}")
                    eng.reg_mov(own, g)
                    g = eng.snap(own, donate=True, min_val=0, max_val=groups - 1)
                times = DUE[kind][5 if ph == TAIL else ph if ph < 3 else 3 + (ph - 3) % 2]
                for n, _ in enumerate(phase(eng, kind, ph, q, g, more)):
                    yield START[q.s][ph] + times[n]

        A, B = streams

        def whole(eng, kind):
            merged(*[run_phases(eng, kind, q, [(ph, 0, True) for ph in range(LEAD[q.s])]) for q in streams])

            def period(i, last):
                tracks = []
                for q in streams:
                    late = [(ph, i, not last) for ph in range(LEAD[q.s], PHASES)]
                    early = [] if last else [(ph, i + 1, True) for ph in range(LEAD[q.s])]
                    tracks += [run_phases(eng, kind, q, late + early), run_phases(eng, kind, q, [(TAIL, i, False)])]
                merged(*tracks)

            with eng.Fori(0, groups - 1) as i:
                period(i, False)
            period(groups - 1, True)

        @block.sync
        def _(sp):
            prep_sync(sp)
            for q in (B, A):
                sync_load(sp, q, 0)
                sp.sem_inc(q.sig["out"].sem, 1)
            whole(sp, "sync")
            for q in (A, B):
                sp.wait_ge(q.sig["out"].sem, 16 * groups + 1)

        @block.gpsimd
        def _(pool):
            prep_gpsimd(pool)
            pool.wait_ge(consts, 1)
            whole(pool, "gpsimd")

        @block.scalar
        def _(act):
            prep_scalar(act)
            act.wait_ge(consts, 1)
            whole(act, "scalar")

        @block.vector
        def _(dve):
            prep_vector(dve)
            dve.wait_ge(consts, 1)
            whole(dve, "vector")

        @block.tensor
        def _(pe):
            prep_tensor(pe)
            pe.wait_ge(consts, 1)
            pe.wait_ge(ident_ready, 3)
            whole(pe, "tensor")


_SMALL = (("L0_gnn_Wq", "L0_gnn_Wk"), ("L0_gnn_Wv", "L0_gnn_Wo"), ("L1_gnn_W", "L2_gnn_W^T"), ("L2_gnn_W", "L2_gnn_attn"))


def kernel(**inputs):
    import numpy as np
    import concourse.bacc as bacc
    from concourse.bass_utils import run_bass_kernel_spmd as run

    a = {k: np.asarray(v) for k, v in inputs.items()}
    x = a["x"]
    B, n, d = x.shape

    def by_partition(v):
        return v.reshape(-1, P).T

    get = lambda name: a[name[:-2]].T if name.endswith("^T") else a[name]
    w = a["L3_gnn_attn_w"]
    cols = np.concatenate([
        by_partition(a["L3_gnn_b1"]), by_partition(a["L3_gnn_beta1"]), by_partition(a["L3_gnn_g1"]),
        by_partition(a["L2_gnn_b"]), np.broadcast_to(a["L3_gnn_attn_b"], (P, L))], axis=1)
    rows = np.concatenate([
        w[:, :d], w[:, d:], a["L3_gnn_g1"], a["L3_gnn_beta1"], a["L3_gnn_g2"], a["L3_gnn_beta2"],
        a["L1_gnn_a"][d:].reshape(1, d), a["L2_gnn_b"].reshape(1, d)], axis=0)
    prep_rows = np.concatenate([a["L1_gnn_a"][:d].reshape(1, d), a["L3_gnn_b2"]], axis=0)
    arrays = {
        "x_in": x.reshape(B * n, d),
        "adj_in": a["adj"].reshape(B * n, n),
        "w_small": np.stack([np.concatenate([get(u), get(v)], axis=0) for u, v in _SMALL]),
        "w1": a["L3_gnn_W1"],
        "w2": a["L3_gnn_W2"],
        "cols": cols,
        "rows": rows,
        "prep_rows": prep_rows,
    }
    arrays = {k: np.ascontiguousarray(v) for k, v in arrays.items()}
    nc = bacc.Bacc("TRN2", target_bir_lowering=False, num_devices=1)
    args = [nc.dram_tensor(k, v.shape, mybir.dt.from_np(v.dtype), kind="ExternalInput").ap() for k, v in arrays.items()]
    out = nc.dram_tensor("out", (B * n, d), F32, kind="ExternalOutput").ap()
    gnn_kernel(nc, *args, out)
    r = run(nc, [arrays], core_ids=[0])
    return r.results[0]["out"].reshape(B, n, d)
```
